# Optimizing a Trainium2 kernel written in Bass

```python
import numpy as np
import jax
import jax.numpy as jnp

def _softmax(x, axis=-1):
    return jax.nn.softmax(x, axis=axis)

def _gelu(x):
    return jax.nn.gelu(x, approximate=True)

def _silu(x):
    return jax.nn.silu(x)

def _sigmoid(x):
    return jax.nn.sigmoid(x)

def _layernorm(x, axis=-1, eps=1e-05):
    m = jnp.mean(x, axis=axis, keepdims=True)
    v = jnp.var(x, axis=axis, keepdims=True)
    return (x - m) / jnp.sqrt(v + eps)

def _scatter_add(tgt, idx, src, axis=0):
    return tgt.at[idx].add(src)

def _segment_sum(src, seg, n):
    return jax.ops.segment_sum(src, seg, n)
kernel_name = 'mk_audio_tower_d1_tok_audfeat1024_r4_9bf7d6'

def setup_inputs(seed: int=0):
    np.random.seed(seed)
    _w = jnp.asarray

    def _rec_inputs():
        import jax
        import jax.numpy as jnp
        _rk = jax.random.key(seed)
        x = -0.000105767 + 0.999885 * jax.random.normal(jax.random.fold_in(_rk, 1), (16, 256, 256), jnp.float32)
        return x
    x = _rec_inputs()

    def _L0_tok_setup():
        import jax, jax.numpy as jnp
        import numpy as np
        B, NP1, D = (64, 577, 256)
        key = jax.random.key(seed)
        k1, k2, k3 = jax.random.split(key, 3)
        X = jax.random.normal(k1, (B, NP1, D), dtype=jnp.float32)
        W = jax.random.normal(k2, (2 * D, D), dtype=jnp.float32) * (1.0 / np.sqrt(2 * D))
        b = jax.random.normal(k3, (D,), dtype=jnp.float32) * 0.01
        return {'X': X, 'W': W, 'b': b}
    _L0_tok_all = _L0_tok_setup()
    _L0_tok_in = {k: v for k, v in _L0_tok_all.items() if k in ('W', 'b')}
    del _L0_tok_all

    def _L0_attn_setup():
        import jax, jax.numpy as jnp
        import numpy as np
        DIM = 256
        HEADS = 16
        DIM_HEAD = 64
        INNER = HEADS * DIM_HEAD
        EPS = 1e-10

        def safe_softmax(s):
            m = jnp.max(s, axis=-1, keepdims=True)
            e = jnp.exp(s - m)
            return e / (jnp.sum(e, axis=-1, keepdims=True) + EPS)
        key = jax.random.key(seed)
        ks = jax.random.split(key, 6)
        B, N = (4, 512)
        x = jax.random.normal(ks[0], (B, N, DIM), dtype=jnp.float32)
        s_in = 1.0 / np.sqrt(DIM)
        s_inner = 1.0 / np.sqrt(INNER)
        Wq = jax.random.uniform(ks[1], (INNER, DIM), jnp.float32, -s_in, s_in)
        Wk = jax.random.uniform(ks[2], (INNER, DIM), jnp.float32, -s_in, s_in)
        Wv = jax.random.uniform(ks[3], (INNER, DIM), jnp.float32, -s_in, s_in)
        Wo = jax.random.uniform(ks[4], (DIM, INNER), jnp.float32, -s_inner, s_inner)
        bo = jax.random.uniform(ks[5], (DIM,), jnp.float32, -s_inner, s_inner)
        return {'x': x, 'Wq': Wq, 'Wk': Wk, 'Wv': Wv, 'Wo': Wo, 'bo': bo}
    _L0_attn_all = _L0_attn_setup()
    _L0_attn_in = {k: v for k, v in _L0_attn_all.items() if k in ('Wq', 'Wk', 'Wv', 'Wo', 'bo')}
    del _L0_attn_all

    def _L0_ffn_setup():
        import jax, jax.numpy as jnp
        import numpy as np
        D = 256
        F = 256
        E = 8
        K = 2
        B, T = (2, 512)

        def _moe_forward(x, router_w, w1, w2, shared_gate_up, shared_down, shared_gate_w):
            b, t, d = x.shape
            xf = x.reshape(-1, d)
            n = xf.shape[0]
            logits = xf @ router_w
            probs = jax.nn.softmax(logits, axis=-1)
            topw, topi = jax.lax.top_k(probs, K)
            combine = jnp.zeros((n, E), dtype=probs.dtype).at[jnp.arange(n)[:, None], topi].add(topw)
            h = jax.nn.silu(jnp.einsum('nd,edf->nef', xf, w1))
            ye = jnp.einsum('nef,efd->ned', h, w2)
            routed = jnp.einsum('ne,ned->nd', combine, ye)
            gu = xf @ shared_gate_up
            gate, up = (gu[:, :F], gu[:, F:])
            shared = jax.nn.silu(gate) * up @ shared_down
            shared = jax.nn.sigmoid(xf @ shared_gate_w) * shared
            return (routed + shared).reshape(b, t, d)
        key = jax.random.key(seed)
        ks = jax.random.split(key, 7)
        std = 0.02
        x = jax.random.normal(ks[0], (B, T, D), dtype=jnp.float32)
        router_w = jax.random.normal(ks[1], (D, E), dtype=jnp.float32) * std
        w1 = jax.random.normal(ks[2], (E, D, F), dtype=jnp.float32) * std
        w2 = jax.random.normal(ks[3], (E, F, D), dtype=jnp.float32) * std
        shared_gate_up = jax.random.normal(ks[4], (D, 2 * F), dtype=jnp.float32) * std
        shared_down = jax.random.normal(ks[5], (F, D), dtype=jnp.float32) * std
        shared_gate_w = jax.random.normal(ks[6], (D, 1), dtype=jnp.float32) * std
        return {'x': x, 'router_w': router_w, 'w1': w1, 'w2': w2, 'shared_gate_up': shared_gate_up, 'shared_down': shared_down, 'shared_gate_w': shared_gate_w}
    _L0_ffn_all = _L0_ffn_setup()
    _L0_ffn_in = {k: v for k, v in _L0_ffn_all.items() if k in ('router_w', 'w1', 'w2', 'shared_gate_up', 'shared_down', 'shared_gate_w')}
    del _L0_ffn_all
    return {'x': x, 'L0_tok_W': _L0_tok_in['W'], 'L0_tok_b': _L0_tok_in['b'], 'L0_attn_Wq': _L0_attn_in['Wq'], 'L0_attn_Wk': _L0_attn_in['Wk'], 'L0_attn_Wv': _L0_attn_in['Wv'], 'L0_attn_Wo': _L0_attn_in['Wo'], 'L0_attn_bo': _L0_attn_in['bo'], 'L0_ffn_router_w': _L0_ffn_in['router_w'], 'L0_ffn_w1': _L0_ffn_in['w1'], 'L0_ffn_w2': _L0_ffn_in['w2'], 'L0_ffn_shared_gate_up': _L0_ffn_in['shared_gate_up'], 'L0_ffn_shared_down': _L0_ffn_in['shared_down'], 'L0_ffn_shared_gate_w': _L0_ffn_in['shared_gate_w']}

def reference(x, L0_tok_W, L0_tok_b, L0_attn_Wq, L0_attn_Wk, L0_attn_Wv, L0_attn_Wo, L0_attn_bo, L0_ffn_router_w, L0_ffn_w1, L0_ffn_w2, L0_ffn_shared_gate_up, L0_ffn_shared_down, L0_ffn_shared_gate_w):
    import jax
    import jax.numpy as jnp

    def _L0_tok_ref(X, W, b):
        import jax, jax.numpy as jnp
        import numpy as np
        B, NP1, D = (64, 577, 256)
        readout = X[:, :1, :]
        other = X[:, 1:, :]
        d = other.shape[-1]
        W1, W2 = (W[:d], W[d:])
        proj = jnp.einsum('bpd,de->bpe', other, W1) + jnp.einsum('bod,de->boe', readout, W2) + b
        return jax.nn.gelu(proj, approximate=False)

    def _L0_attn_ref(x, Wq, Wk, Wv, Wo, bo):
        import jax, jax.numpy as jnp
        import numpy as np
        DIM = 256
        HEADS = 16
        DIM_HEAD = 64
        INNER = HEADS * DIM_HEAD
        EPS = 1e-10

        def safe_softmax(s):
            m = jnp.max(s, axis=-1, keepdims=True)
            e = jnp.exp(s - m)
            return e / (jnp.sum(e, axis=-1, keepdims=True) + EPS)
        B, N, _ = x.shape
        scale = DIM_HEAD ** (-0.5)

        def split_heads(t):
            return t.reshape(B, N, HEADS, DIM_HEAD).transpose(0, 2, 1, 3)
        q = split_heads(x @ Wq.T)
        k = split_heads(x @ Wk.T)
        v = split_heads(x @ Wv.T)
        sim = jnp.einsum('bhid,bhjd->bhij', q, k) * scale
        attn = safe_softmax(sim)
        out = jnp.einsum('bhij,bhjd->bhid', attn, v)
        out = out.transpose(0, 2, 1, 3).reshape(B, N, INNER)
        return out @ Wo.T + bo

    def _L0_ffn_ref(x, router_w, w1, w2, shared_gate_up, shared_down, shared_gate_w):
        import jax, jax.numpy as jnp
        import numpy as np
        D = 256
        F = 256
        E = 8
        K = 2
        B, T = (2, 512)

        def _moe_forward(x, router_w, w1, w2, shared_gate_up, shared_down, shared_gate_w):
            b, t, d = x.shape
            xf = x.reshape(-1, d)
            n = xf.shape[0]
            logits = xf @ router_w
            probs = jax.nn.softmax(logits, axis=-1)
            topw, topi = jax.lax.top_k(probs, K)
            combine = jnp.zeros((n, E), dtype=probs.dtype).at[jnp.arange(n)[:, None], topi].add(topw)
            h = jax.nn.silu(jnp.einsum('nd,edf->nef', xf, w1))
            ye = jnp.einsum('nef,efd->ned', h, w2)
            routed = jnp.einsum('ne,ned->nd', combine, ye)
            gu = xf @ shared_gate_up
            gate, up = (gu[:, :F], gu[:, F:])
            shared = jax.nn.silu(gate) * up @ shared_down
            shared = jax.nn.sigmoid(xf @ shared_gate_w) * shared
            return (routed + shared).reshape(b, t, d)
        return _moe_forward(x, router_w, w1, w2, shared_gate_up, shared_down, shared_gate_w)
    h = _L0_tok_ref(x, L0_tok_W, L0_tok_b)
    h = h + _L0_attn_ref(_layernorm(h, axis=-1), L0_attn_Wq, L0_attn_Wk, L0_attn_Wv, L0_attn_Wo, L0_attn_bo)
    h = h + _L0_ffn_ref(_layernorm(h, axis=-1), L0_ffn_router_w, L0_ffn_w1, L0_ffn_w2, L0_ffn_shared_gate_up, L0_ffn_shared_down, L0_ffn_shared_gate_w)
    return h

_drawn_inputs = setup_inputs


def setup_inputs(seed=0):
    import zlib

    import numpy as np

    out = dict(_drawn_inputs(seed))
    spreads = {}
    factors = {'L0_tok_b': 5.062,
     'L0_attn_Wq': 5.184,
     'L0_attn_Wk': 4.934,
     'L0_ffn_router_w': 3.38,
     'L0_ffn_w1': 3.031,
     'L0_ffn_w2': 2.984,
     'L0_ffn_shared_gate_up': 4.589,
     'L0_ffn_shared_down': 4.598,
     'L0_ffn_shared_gate_w': 8.0}
    for name, (base, spread) in spreads.items():
        noise = np.random.default_rng([zlib.crc32(name.encode()), seed]).standard_normal(out[name].shape)
        drawn = base * np.exp(spread * noise) if base else spread * noise
        out[name] = jnp.asarray(drawn.astype(out[name].dtype))
    for name, factor in factors.items():
        out[name] = (out[name] * factor).astype(out[name].dtype)
    return out
```

```python
from contextlib import ExitStack

import concourse.bass as bass
from concourse import mybir

P = 128
B, N, D = 16, 256, 256
DC = D // P
HEADS, DH = 16, 64
INNER = HEADS * DH
PAIRS = HEADS // 2
GROUPS = B // 2
GT = 4
GR = GT * P
E, F = 8, 256
FC = F // P
UNITS = 2 * PAIRS
SCALE = DH ** -0.5
EPS_LN, EPS_SM = 1e-5, 1e-10

ALU = mybir.AluOpType
ACT = mybir.ActivationFunctionType
F32 = mybir.dt.float32
F32R = mybir.dt.float32r
U32 = mybir.dt.uint32
AX_X = mybir.AxisListType.X


def f32(ap):
    return ap.bitcast(F32)


def three(pe, out, wh, wl, xh, xl, start, stop):
    pe.matmul(out, wl, xh, start=start, stop=False, skip_group_check=True)
    pe.matmul(out, wh, xl, start=False, stop=False, skip_group_check=True)
    return pe.matmul(out, wh, xh, start=False, stop=stop, skip_group_check=True)


def build(nc, x, tok_w, tok_b, wq, wk, wv, wo, bo, router_w, w1, w2, gate_up, down, gate_w, out):
    x_rows = x.rearrange("b (h p) d -> p (b h) d", p=P)
    with ExitStack() as ctx:
        resid = ctx.enter_context(nc.sbuf_tensor("resid", [P, B * N // P, D], F32))
        ident = ctx.enter_context(nc.sbuf_tensor("ident", [P, P], F32))
        half_neg = ctx.enter_context(nc.sbuf_tensor("half_neg", [P, GT], F32))
        with ExitStack() as weights:
            qkv_parts = [weights.enter_context(nc.sbuf_tensor(n, [P, DC, INNER], F32R))
                         for n in ("wq_hi", "wq_lo", "wk_hi", "wk_lo", "wv_hi", "wv_lo")]
            wo_parts = [weights.enter_context(nc.sbuf_tensor(n, [P, PAIRS, D], F32R))
                        for n in ("wo_hi", "wo_lo")]
            token_phase(nc, x, x_rows, tok_w, tok_b, wq, wk, wv, wo, resid, ident, half_neg,
                        qkv_parts, wo_parts)
            attention_phase(nc, bo, resid, ident, half_neg, qkv_parts, wo_parts)
        moe_phase(nc, router_w, w1, w2, gate_up, down, gate_w, out, resid, ident, half_neg)


def token_phase(nc, x, x_rows, tok_w, tok_b, wq, wk, wv, wo, resid, ident, half_neg,
                qkv_parts, wo_parts):
    with ExitStack() as ctx:
        def sb(name, shape, dt=F32):
            return ctx.enter_context(nc.sbuf_tensor(name, shape, dt))

        def sem(name):
            return ctx.enter_context(nc.semaphore(name))

        xin = [sb(f"xin{i}", [P, GT, D]) for i in range(2)]
        xT_hi, xT_lo = (sb(n, [P, DC, GR], F32R) for n in ("xT_hi", "xT_lo"))
        hT = sb("hT", [P, DC, GR])
        raw = [sb(f"raw_{n}", [P, INNER // P, D]) for n in "qkv"]
        raw_o = sb("raw_o", [P, DC, INNER])
        tokw = sb("tokw", [P, 2 * DC, D])
        tokw_hi, tokw_lo = (sb(n, [P, DC, D], F32R) for n in ("tokw_hi", "tokw_lo"))
        ro = sb("ro", [B, D])
        roT = sb("roT", [P, DC, B])
        bcol = sb("bcol", [P, DC])
        rbias = sb("rbias", [P, DC, B])
        xT_ps = [ctx.enter_context(nc.psum_tensor(f"xT_ps{c}", [P, 512], F32)) for c in range(2)]
        tok_ps = [ctx.enter_context(nc.psum_tensor(f"tok_ps{c}", [P, 512], F32)) for c in range(2)]
        h_ps = [ctx.enter_context(nc.psum_tensor(f"h_ps{c}", [P, 512], F32)) for c in range(2)]
        w_ps = [ctx.enter_context(nc.psum_tensor(f"w_ps{c}", [P, 512], F32)) for c in range(2)]

        x_in = [sem(f"x_in{i}") for i in range(2)]
        s_ro, s_tokw, s_bcol = sem("ro_in"), sem("tokw_in"), sem("bcol_in")
        s_raw = [sem(f"raw_in{i}") for i in range(4)]
        s_zero, s_ident, s_half = sem("ident_zeroed"), sem("ident_ready"), sem("half_ready")
        s_roT_ps, s_roT, s_r_ps, s_rbias = sem("roT_ps"), sem("roT_ready"), sem("r_ps"), sem("rbias")
        s_tw_hi, s_tw_lo = sem("tokw_hi_ready"), sem("tokw_lo_ready")
        s_xT_ps, s_xT_hi, s_xT_lo = sem("xT_in_psum"), sem("xT_hi_ready"), sem("xT_lo_ready")
        s_tok, s_gelu = sem("tok_in_psum"), sem("hT_ready")
        s_h, s_res = sem("h_in_psum"), sem("resid_written")
        s_w, s_w_hi, s_w_lo = sem("w_in_psum"), sem("w_hi_ready"), sem("w_lo_ready")

        banks = []
        for w in range(3):
            for c in range(DC):
                for half in range(2):
                    src = [(raw[w][:, 4 * half + r, c * P:(c + 1) * P]) for r in range(4)]
                    dst = [qkv_parts[2 * w + k][:, c, 512 * half:512 * half + 512] for k in range(2)]
                    banks.append((w, src, dst, SCALE if w == 0 else 1.0))
        for pp in range(0, PAIRS, 2):
            src = [raw_o[:, c, (pp + i) * P:(pp + i + 1) * P] for i in range(2) for c in range(DC)]
            dst = [wo_parts[k][:, pp:pp + 2, :] for k in range(2)]
            banks.append((3, src, dst, 1.0))
        per_group = len(banks) // GROUPS

        block = ctx.enter_context(nc.Block())

        @block.sync
        def _(sp):
            sp.dma_start(ro[:], x[:, 0, :]).then_inc(s_ro, 16)
            sp.dma_start(tokw[:], tok_w.rearrange("(c p) e -> p c e", p=P)).then_inc(s_tokw, 16)
            sp.dma_start(xin[0][:], x_rows[:, 0:GT, :]).then_inc(x_in[0], 16)
            sp.dma_start(xin[1][:], x_rows[:, GT:2 * GT, :]).then_inc(x_in[1], 16)
            for i, w in enumerate((wq, wk, wv)):
                sp.dma_start(raw[i][:], w.rearrange("(r p) d -> p r d", p=P)).then_inc(s_raw[i], 16)
            sp.dma_start(raw_o[:], wo.rearrange("(c p) i -> p c i", p=P)).then_inc(s_raw[3], 16)
            for g in range(2, GROUPS):
                sp.wait_ge(s_xT_ps, DC * (g - 1))
                sp.dma_start(xin[g % 2][:], x_rows[:, GT * g:GT * g + GT, :]).then_inc(x_in[g % 2], 16)

        @block.gpsimd
        def _(pool):
            pool.memset(ident[:], 0.0).then_inc(s_zero, 1)
            pool.memset(half_neg[:], -0.5).then_inc(s_half, 1)
            pool.wait_ge(s_zero, 1)
            pool.affine_select(out=ident[:], in_=ident[:], compare_op=ALU.not_equal, fill=1.0, base=0,
                               pattern=[[-1, P]], channel_multiplier=1).then_inc(s_ident, 1)

        def transpose_x(pe, g):
            k = g % 2
            pe.wait_ge(x_in[k], 16 * (g // 2 + 1))
            for c in range(DC):
                for t in range(GT):
                    m = pe.transpose(xT_ps[c][:, t * P:(t + 1) * P], xin[k][:, t, c * P:(c + 1) * P], ident[:])
                m.then_inc(s_xT_ps, 1)

        @block.tensor
        def _(pe):
            pe.wait_ge(s_ident, 1)
            pe.wait_ge(s_ro, 16)
            for c in range(DC):
                m = pe.transpose(h_ps[0][:, c * B:(c + 1) * B], ro[:, c * P:(c + 1) * P], ident[:B, :B])
            m.then_inc(s_roT_ps, 1)
            transpose_x(pe, 0)
            pe.wait_ge(s_roT, 1)
            pe.wait_ge(s_tokw, 16)
            for e in range(DC):
                for c in range(DC):
                    m = pe.matmul(h_ps[1][:, e * B:(e + 1) * B], tokw[:, DC + c, e * P:(e + 1) * P], roT[:, c, :],
                                  start=c == 0, stop=c == DC - 1)
            m.then_inc(s_r_ps, 1)

            def group(g, last):
                pe.wait_ge(s_xT_lo, DC * g + DC)
                if g == 0:
                    pe.wait_ge(s_tw_lo, 1)
                else:
                    pe.wait_ge(s_gelu, 4 * g)
                for e in range(DC):
                    for c in range(DC):
                        m = three(pe, tok_ps[e][:], tokw_hi[:, c, e * P:(e + 1) * P],
                                  tokw_lo[:, c, e * P:(e + 1) * P], xT_hi[:, c, :], xT_lo[:, c, :],
                                  c == 0, c == DC - 1)
                    m.then_inc(s_tok, 1)
                if not last:
                    transpose_x(pe, g + 1)

            def weights(g):
                for j in range(per_group):
                    n = per_group * g + j
                    which, src, _, _ = banks[n]
                    pe.wait_ge(s_raw[which], 16)
                    if n >= 2:
                        pe.wait_ge(s_w_lo, n - 1)
                    for i, s in enumerate(src):
                        m = pe.transpose(w_ps[j][:, i * P:(i + 1) * P], s, ident[:])
                    m.then_inc(s_w, 1)

            def rows(g):
                pe.wait_ge(s_gelu, 4 * g + 4)
                if g == 0:
                    pe.wait_ge(s_rbias, 1)
                else:
                    pe.wait_ge(s_res, 2 * g)
                for j in range(2):
                    for t in range(2):
                        for c in range(DC):
                            o = t * D + c * P
                            m = pe.transpose(h_ps[j][:, o:o + P], hT[:, c, (2 * j + t) * P:(2 * j + t + 1) * P], ident[:])
                    m.then_inc(s_h, 1)

            for g in range(GROUPS):
                group(g, g == GROUPS - 1)
                weights(g)
                rows(g)

        @block.scalar
        def _(act):
            act.dma_start(bcol[:], tok_b.rearrange("(c p) -> p c", p=P), allow_slow_non_contiguous=True).then_inc(s_bcol, 16)
            act.wait_ge(s_tokw, 16)
            act.activation(tokw_hi[:], tokw[:, 0:DC, :], ACT.Copy).then_inc(s_tw_hi, 1)

            def x_hi(g):
                for c in range(DC):
                    act.wait_ge(s_xT_ps, DC * g + c + 1)
                    if g:
                        act.wait_ge(s_tok, DC * g)
                    act.activation(xT_hi[:, c, :], xT_ps[c][:], ACT.Copy).then_inc(s_xT_hi, 1)

            x_hi(0)
            for g in range(GROUPS):
                if g + 1 < GROUPS:
                    x_hi(g + 1)
                if g == 0:
                    act.wait_ge(s_rbias, 1)
                for e in range(DC):
                    act.wait_ge(s_tok, DC * g + e + 1)
                    if g and e == 0:
                        act.wait_ge(s_h, 2 * g)
                    for b in range(2):
                        n = 2 * g + b
                        act.activation(hT[:, e, b * N:(b + 1) * N], tok_ps[e][:, b * N:(b + 1) * N], ACT.Gelu,
                                       bias=rbias[:, e, n:n + 1]).then_inc(s_gelu, 1)
                for j in range(per_group):
                    n = per_group * g + j
                    act.wait_ge(s_w, n + 1)
                    hi = banks[n][2][0]
                    src = w_ps[j][:] if banks[n][0] < 3 else w_ps[j][:].rearrange("p (i d) -> p i d", i=2)
                    act.activation(hi, src, ACT.Copy, scale=banks[n][3]).then_inc(s_w_hi, 1)

        @block.vector
        def _(dve):
            dve.wait_ge(s_roT_ps, 1)
            dve.tensor_copy(roT[:], h_ps[0][:, 0:DC * B].rearrange("p (c b) -> p c b", c=DC)).then_inc(s_roT, 1)
            dve.wait_ge(s_tw_hi, 1)
            dve.tensor_tensor(tokw_lo[:], tokw[:, 0:DC, :], f32(tokw_hi[:]), ALU.subtract).then_inc(s_tw_lo, 1)
            dve.wait_ge(s_r_ps, 1)
            dve.wait_ge(s_bcol, 16)
            for e in range(DC):
                m = dve.tensor_scalar(rbias[:, e, :], h_ps[1][:, e * B:(e + 1) * B], bcol[:, e:e + 1], None, ALU.add)
            m.then_inc(s_rbias, 1)

            def x_lo(g):
                for c in range(DC):
                    dve.wait_ge(s_xT_hi, DC * g + c + 1)
                    dve.tensor_tensor(xT_lo[:, c, :], xT_ps[c][:], f32(xT_hi[:, c, :]), ALU.subtract).then_inc(s_xT_lo, 1)

            x_lo(0)
            for g in range(GROUPS):
                if g + 1 < GROUPS:
                    x_lo(g + 1)
                for j in range(per_group):
                    n = per_group * g + j
                    dve.wait_ge(s_w_hi, n + 1)
                    hi, lo = banks[n][2]
                    src = w_ps[j][:] if banks[n][0] < 3 else w_ps[j][:].rearrange("p (i d) -> p i d", i=2)
                    dve.scalar_tensor_tensor(out=lo, in0=src, scalar=banks[n][3], in1=f32(hi), op0=ALU.mult,
                                             op1=ALU.subtract).then_inc(s_w_lo, 1)
                for j in range(2):
                    dve.wait_ge(s_h, 2 * g + j + 1)
                    dve.tensor_copy(resid[:, GT * g + 2 * j:GT * g + 2 * j + 2, :],
                                    h_ps[j][:].rearrange("p (t d) -> p t d", t=2)).then_inc(s_res, 1)


def attention_phase(nc, bo, resid, ident, half_neg, qkv_parts, wo_parts):
    wq_hi, wq_lo, wk_hi, wk_lo, wv_hi, wv_lo = qkv_parts
    wo_hi, wo_lo = wo_parts
    with ExitStack() as ctx:
        def sb(name, shape, dt=F32):
            return ctx.enter_context(nc.sbuf_tensor(name, shape, dt))

        def bank(name):
            return ctx.enter_context(nc.psum_tensor(name, [P, 512], F32))

        def sem(name):
            return ctx.enter_context(nc.semaphore(name))

        bo_row = sb("bo_row", [P, D])
        z = sb("z", [P, GT, D])
        zT_hi, zT_lo = (sb(n, [P, DC, GR], F32R) for n in ("zT_hi", "zT_lo"))
        qk = [[[sb(f"{n}_{part}{i}", [P, GR], F32R) for part in ("hi", "lo")] for n in "qk"] for i in range(2)]
        v = [sb(f"v{i}", [P, GT, 2 * P]) for i in range(2)]
        prob = [sb(f"prob{i}", [P, 2, 2, N]) for i in range(2)]
        probT = [sb(f"probT{i}", [P, 2, 2, N]) for i in range(2)]
        oT_hi, oT_lo = (sb(n, [P, PAIRS, GR], F32R) for n in ("oT_hi", "oT_lo"))
        nmax = [sb(f"nmax{i}", [P, 4]) for i in range(2)]
        rsum = [sb(f"rsum{i}", [P, 4]) for i in range(2)]
        rsum_eps = sb("rsum_eps", [P, 4])
        rinv = [sb(f"rinv{i}", [P, 4]) for i in range(2)]
        stats = sb("stats", [P, GT, 6])
        mean_var = sb("mean_var", [P, GT, 2])
        var_eps = sb("var_eps", [P, GT])
        rstd = sb("rstd", [P, GT])
        s_ps = [bank(f"s_ps{h}") for h in range(2)]
        pT_ps = [bank(f"pT_ps{h}") for h in range(2)]
        o_ps = bank("o_ps")
        proj_ps = [bank(f"proj_ps{j}") for j in range(2)]
        v_ps = bank("v_ps")

        s_bo = sem("bo_in")
        s_mask = sem("masked_key_zeroed")
        s_S, s_max, s_exp = sem("scores"), sem("neg_max"), sem("exps")
        s_sum, s_rinv, s_nA, s_nB = sem("sum_eps"), sem("sum_inverse"), sem("normal_A"), sem("normal_B")
        s_T, s_pA, s_pB = sem("transposed"), sem("probT_A"), sem("probT_B")
        s_o, s_oh, s_ol = sem("o_in_psum"), sem("oT_hi_ready"), sem("oT_lo_ready")
        s_qk, s_qkh, s_qkl = sem("qk_in_psum"), sem("qk_hi_ready"), sem("qk_lo_ready")
        s_v, s_ve = sem("v_in_psum"), sem("v_ready")
        s_zt, s_zh, s_zl = sem("zT_in_psum"), sem("zT_hi2"), sem("zT_lo2")
        s_st, s_mv, s_var, s_rstd, s_z, s_bias = (sem("bn_stats"), sem("mean_var"), sem("var_eps"), sem("rstd"),
                                                  sem("z_ready"), sem("bo_added"))
        s_wo, s_woe = sem("out_rows_in_psum"), sem("out_rows_added")
        s_go, s_pgo = sem("vector_wait_met"), sem("pool_wait_met")

        FREE_P = 4
        FREE_B = 1
        FREE_W = 2

        block = ctx.enter_context(nc.Block())

        @block.sync
        def _(sp):
            sp.dma_start(bo_row[:], bo.rearrange("(a d) -> a d", a=1).broadcast_to([P, D])).then_inc(s_bo, 16)


        @block.tensor
        def _(pe):
            pe.sem_inc(s_T, FREE_P)

            def transpose_z(g, free):
                pe.wait_ge(s_z, GT * g + GT)
                for c in range(DC):
                    if free:
                        pe.wait_ge(s_qkl, UNITS * g - 1 + c)
                    for t in range(GT):
                        m = pe.transpose(proj_ps[c][:, t * P:(t + 1) * P], z[:, t, c * P:(c + 1) * P], ident[:])
                    m.then_inc(s_zt, 1)

            def project_qk(g, j):
                hi, lo = (wq_hi, wq_lo) if j % 2 == 0 else (wk_hi, wk_lo)
                cols = slice((j // 2) * P, (j // 2 + 1) * P)
                for c in range(DC):
                    m = three(pe, proj_ps[j % 2][:], hi[:, c, cols], lo[:, c, cols], zT_hi[:, c, :], zT_lo[:, c, :],
                              c == 0, c == DC - 1)
                m.then_inc(s_qk, 1)

            def project_v(g, j):
                t, cols = j % 4, slice((j // 4) * 2 * P, (j // 4 + 1) * 2 * P)
                rows = slice(t * P, (t + 1) * P)
                for c in range(DC):
                    m = three(pe, v_ps[:, 0:2 * P], zT_hi[:, c, rows], zT_lo[:, c, rows], wv_hi[:, c, cols],
                              wv_lo[:, c, cols], c == 0, c == DC - 1)
                m.then_inc(s_v, 1)

            def scores(g, i, free):
                u, pair, b = UNITS * g + i, i // 2, i % 2
                (q_hi, q_lo), (k_hi, k_lo) = qk[pair % 2]
                pe.wait_ge(s_qkl, UNITS * g + 2 * pair + 2)
                if free:
                    pe.wait_ge(s_exp, 2 * u)
                keys = slice(b * N, (b + 1) * N)
                for qt in range(2):
                    rows = slice(b * N + qt * P, b * N + (qt + 1) * P)
                    for n, (a, k) in enumerate(((q_lo, k_hi), (q_hi, k_lo), (q_hi, k_hi))):
                        for h in range(2):
                            part = slice(h * DH, (h + 1) * DH)
                            m = pe.matmul(s_ps[h][:, qt * N:(qt + 1) * N], a[part, rows], k[part, keys],
                                          start=n == 0, stop=n == 2)
                            if qt == 1 and n == 2:
                                m.then_inc(s_S, 1)

            def transpose_p(g, i):
                u = UNITS * g + i
                for h, (normal, free) in enumerate(((s_nA, s_pA), (s_nB, s_pB))):
                    pe.wait_ge(normal, u + 1)
                    pe.wait_ge(free, u + FREE_B)
                    for kt in range(2):
                        for qt in range(2):
                            o = kt * N + qt * P
                            m = pe.transpose(pT_ps[h][:, o:o + P], prob[u_par(i)][:, h, qt, kt * P:(kt + 1) * P], ident[:])
                    m.then_inc(s_T, 1)

            def values(g, i):
                u, pair, b = UNITS * g + i, i // 2, i % 2
                pe.wait_ge(s_ve, UNITS * g + 4 * (pair // 2) + 4)
                pe.wait_ge(s_ol, u + FREE_B)
                pe.wait_ge(s_pA, u + 1 + FREE_B)
                pe.wait_ge(s_pB, u + 1 + FREE_B)
                vt = v[(pair // 2) % 2]
                for kt in range(2):
                    for h in range(2):
                        col = (pair % 2) * P + h * DH
                        m = pe.matmul(o_ps[h * DH:(h + 1) * DH, 0:N], vt[:, 2 * b + kt, col:col + DH],
                                      probT[u_par(i)][:, h, kt, :], start=kt == 0, stop=kt == 1)
                m.then_inc(s_o, 1)

            def output_rows(g, last):
                for j in range(2):
                    pe.wait_ge(s_ol, UNITS * g + UNITS - 1 + j + FREE_B)
                    pe.wait_ge(s_qkl, UNITS * g + UNITS + (-1 if last else 3) + j)
                    for t in (2 * j, 2 * j + 1):
                        rows = slice(t * P, (t + 1) * P)
                        for pair in range(PAIRS):
                            m = three(pe, proj_ps[j][:, (t % 2) * D:(t % 2 + 1) * D], oT_hi[:, pair, rows],
                                      oT_lo[:, pair, rows], wo_hi[:, pair, :], wo_lo[:, pair, :],
                                      pair == 0, pair == PAIRS - 1)
                    m.then_inc(s_wo, 1)

            def group(g, last):
                for i in range(UNITS):
                    ahead = i + 4
                    if i == UNITS - 4 and not last:
                        transpose_z(g + 1, True)
                    if i + 1 < UNITS:
                        scores(g, i + 1, True)
                    elif not last:
                        scores(g + 1, 0, True)

                    def next_qk():
                        if ahead >= UNITS and last:
                            return
                        if i < 2:
                            pe.wait_ge(s_woe, 2 * g + i - 1 + FREE_W)
                        pe.wait_ge(s_qkl, UNITS * g + ahead - 1)
                        project_qk(g + ahead // UNITS, ahead % UNITS)

                    def next_v():
                        if ahead < UNITS or not last:
                            pe.wait_ge(s_ve, UNITS * g + ahead)
                            if i == UNITS - 4:
                                pe.wait_ge(s_zl, DC * (g + 2))
                            project_v(g + ahead // UNITS, ahead % UNITS)

                    if i != UNITS - 4:
                        next_v()
                    transpose_p(g, i)
                    if i == UNITS - 4:
                        next_v()
                    next_qk()
                    values(g, i)
                output_rows(g, last)

            transpose_z(0, False)
            pe.wait_ge(s_zl, DC)
            for j in range(4):
                if j >= 2:
                    pe.wait_ge(s_qkl, j - 1)
                project_qk(0, j)
                if j:
                    pe.wait_ge(s_ve, j)
                project_v(0, j)
                if j == 1:
                    scores(0, 0, False)
            with pe.Fori(0, GROUPS - 1) as g:
                group(g, False)
            group(GROUPS - 1, True)

        @block.scalar
        def _(act):
            act.sem_inc(s_pA, FREE_B)

            def exps(g, i, h):
                u = UNITS * g + i
                if h == 0:
                    act.wait_ge(s_T, 2 * u + 2)
                act.wait_ge(s_max, 2 * u + h + 1)
                for qt in range(2):
                    n = 2 * h + qt
                    m = act.activation(prob[u_par(i)][:, h, qt, 1:N], s_ps[h][:, qt * N + 1:(qt + 1) * N], ACT.Exp,
                                       bias=nmax[u_par(i)][:, n:n + 1], accum_out=rsum[u_par(i)][:, n:n + 1])
                m.then_inc(s_exp, 1)

            def qk_hi(g, j):
                act.wait_ge(s_qk, UNITS * g + j + 1)
                act.activation(qk[(j // 2) % 2][j % 2][0][:], proj_ps[j % 2][:], ACT.Copy).then_inc(s_qkh, 1)

            def z_hi(g):
                for c in range(DC):
                    act.wait_ge(s_zt, DC * g + c + 1)
                    act.activation(zT_hi[:, c, :], proj_ps[c][:], ACT.Copy).then_inc(s_zh, 1)

            def probT_a(g, i):
                act.wait_ge(s_T, 2 * (UNITS * g + i) + 1 + FREE_P)
                act.activation(probT[u_par(i)][:, 0, :, :], pT_ps[0][:].rearrange("p (k q) -> p k q", k=2),
                               ACT.Copy).then_inc(s_pA, 1)

            def o_hi(g, i):
                act.wait_ge(s_o, UNITS * g + i + 1)
                act.activation(oT_hi[:, i // 2, (i % 2) * N:(i % 2 + 1) * N], o_ps[:, 0:N], ACT.Copy).then_inc(s_oh, 1)

            def group(g, last):
                for i in range(UNITS):
                    nxt = (g, i + 1) if i + 1 < UNITS else (g + 1, 0)
                    has_next = i + 1 < UNITS or not last
                    tile = (g + (i + 4) // UNITS, (i + 4) % UNITS)
                    has_tile = i + 4 < UNITS or not last
                    if i == UNITS - 4 and not last:
                        z_hi(g + 1)
                    if has_next:
                        exps(*nxt, 0)
                    probT_a(g, i)
                    if has_next:
                        exps(*nxt, 1)
                    if has_tile:
                        qk_hi(*tile)
                    o_hi(g, i)

            z_hi(0)
            act.wait_ge(s_mask, 2)
            for j in range(4):
                qk_hi(0, j)
                if j == 1:
                    exps(0, 0, 0)
                    exps(0, 0, 1)
            with act.Fori(0, GROUPS - 1) as g:
                group(g, False)
            group(GROUPS - 1, True)

        @block.vector
        def _(dve):
            dve.sem_inc(s_pB, FREE_B)
            dve.sem_inc(s_ol, FREE_B)
            dve.sem_inc(s_woe, FREE_W)
            for i in range(2):
                dve.memset(prob[i][:, :, :, 0:1], 0.0).then_inc(s_mask, 1)

            def layernorm_stats(g, t):
                dve.bn_stats(stats[:, t, :], resid[:, GT * g + t, :]).then_inc(s_st, 1)
                dve.wait_ge(s_st, GT * g + t + 1)
                dve.sem_inc(s_go, 1)
                dve.bn_aggr(mean_var[:, t, :], stats[:, t, :]).then_inc(s_mv, 1)

            def layernorm_apply(g, t):
                dve.wait_ge(s_rstd, g + 1)
                dve.tensor_scalar(z[:, t, :], resid[:, GT * g + t, :], mean_var[:, t, 0:1], rstd[:, t:t + 1],
                                  ALU.subtract, ALU.mult).then_inc(s_z, 1)

            def maxima(g, i):
                for h in range(2):
                    dve.wait_ge(s_S, 2 * (UNITS * g + i) + h + 1)
                    dve.tensor_reduce(nmax[u_par(i)][:, 2 * h:2 * h + 2],
                                      s_ps[h][:].rearrange("p (q k) -> p q k", q=2)[:, :, 1:N], AX_X, ALU.max,
                                      negate=True).then_inc(s_max, 1)

            def qk_lo(g, j):
                hi, lo = qk[(j // 2) % 2][j % 2]
                dve.wait_ge(s_qkh, UNITS * g + j + 1)
                dve.tensor_tensor(lo[:], proj_ps[j % 2][:], f32(hi[:]), ALU.subtract).then_inc(s_qkl, 1)

            def z_lo(g):
                for c in range(DC):
                    dve.wait_ge(s_zh, DC * g + c + 1)
                    dve.tensor_tensor(zT_lo[:, c, :], proj_ps[c][:], f32(zT_hi[:, c, :]), ALU.subtract).then_inc(s_zl, 1)

            def v_copy(g, j):
                dve.wait_ge(s_v, UNITS * g + j + 1)
                dve.tensor_copy(v[(j // 4) % 2][:, j % 4, :], v_ps[:, 0:2 * P]).then_inc(s_ve, 1)

            def normalise_a(g, i):
                u, k = UNITS * g + i, u_par(i)
                dve.wait_ge(s_exp, 2 * u + 2)
                dve.tensor_scalar(rsum_eps[:], rsum[k][:], EPS_SM, None, ALU.add).then_inc(s_sum, 1)
                dve.wait_ge(s_sum, u + 1)
                dve.reciprocal(rinv[k][:], rsum_eps[:]).then_inc(s_rinv, 1)
                dve.wait_ge(s_rinv, u + 1)
                for qt in range(2):
                    m = dve.tensor_scalar(prob[k][:, 0, qt, 1:N], prob[k][:, 0, qt, 1:N], rinv[k][:, qt:qt + 1], None,
                                          ALU.mult)
                m.then_inc(s_nA, 1)

            def probT_b(g, i):
                dve.wait_ge(s_T, 2 * (UNITS * g + i) + 2 + FREE_P)
                dve.tensor_copy(probT[u_par(i)][:, 1, :, :],
                                pT_ps[1][:].rearrange("p (k q) -> p k q", k=2)).then_inc(s_pB, 1)

            def o_lo(g, i):
                part = slice((i % 2) * N, (i % 2 + 1) * N)
                dve.wait_ge(s_oh, UNITS * g + i + 1)
                dve.tensor_tensor(oT_lo[:, i // 2, part], o_ps[:, 0:N], f32(oT_hi[:, i // 2, part]),
                                  ALU.subtract).then_inc(s_ol, 1)

            def add_rows(g):
                dve.wait_ge(s_bias, GT * g + GT)
                for j in range(2):
                    rows = resid[:, bass.ds(GT * g + 2 * j, 2), :]
                    dve.wait_ge(s_wo, 2 * g + j + 1)
                    dve.tensor_tensor(rows, proj_ps[j][:].rearrange("p (t d) -> p t d", t=2), rows,
                                      ALU.add).then_inc(s_woe, 1)

            def group(g, last):
                for i in range(UNITS):
                    nxt = (g, i + 1) if i + 1 < UNITS else (g + 1, 0)
                    has_next = i + 1 < UNITS or not last
                    tile = (g + (i + 4) // UNITS, (i + 4) % UNITS)
                    has_tile = i + 4 < UNITS or not last
                    if i == UNITS - 4 and not last:
                        z_lo(g + 1)
                    if has_next:
                        maxima(*nxt)
                    if has_tile and i != UNITS - 4:
                        v_copy(*tile)
                    probT_b(g, i)
                    if has_tile and i == UNITS - 4:
                        v_copy(*tile)
                    if has_next:
                        normalise_a(*nxt)
                    if has_tile:
                        qk_lo(*tile)
                    o_lo(g, i)
                    if not last and 2 <= i < 2 + GT:
                        layernorm_stats(g + 1, i - 2)
                    if not last and 7 <= i < 7 + GT:
                        layernorm_apply(g + 1, i - 7)
                add_rows(g)

            for t in range(GT):
                layernorm_stats(0, t)
            for t in range(GT):
                layernorm_apply(0, t)
            z_lo(0)
            for j in range(4):
                qk_lo(0, j)
                v_copy(0, j)
                if j == 1:
                    maxima(0, 0)
                    normalise_a(0, 0)
            with dve.Fori(0, GROUPS - 1) as g:
                group(g, False)
            group(GROUPS - 1, True)

        @block.gpsimd
        def _(pool):
            def layernorm_rstd(g):
                pool.wait_ge(s_mv, GT * g + GT)
                pool.sem_inc(s_pgo, 1)
                pool.tensor_scalar(var_eps[:], mean_var[:, :, 1], EPS_LN, None, ALU.add).then_inc(s_var, 1)
                pool.wait_ge(s_var, g + 1)
                pool.tensor_tensor(rstd[:], var_eps[:], half_neg[:], ALU.pow).then_inc(s_rstd, 1)

            def add_bias(g, t):
                pool.wait_ge(s_z, GT * g + t + 1)
                rows = resid[:, GT * g + t, :]
                pool.tensor_tensor(rows, rows, bo_row[:], ALU.add).then_inc(s_bias, 1)

            def normalise_b(g, i):
                k = u_par(i)
                pool.wait_ge(s_rinv, UNITS * g + i + 1)
                pool.sem_inc(s_pgo, 1)
                for qt in range(2):
                    m = pool.tensor_scalar(prob[k][:, 1, qt, 1:N], prob[k][:, 1, qt, 1:N], rinv[k][:, 2 + qt:3 + qt],
                                           None, ALU.mult)
                m.then_inc(s_nB, 1)

            def group(g, last):
                for i in range(UNITS):
                    if i + 1 < UNITS:
                        normalise_b(g, i + 1)
                    elif not last:
                        normalise_b(g + 1, 0)
                    if i == 2 + GT and not last:
                        layernorm_rstd(g + 1)
                    if 8 <= i < 8 + GT and not last:
                        add_bias(g + 1, i - 8)

            layernorm_rstd(0)
            pool.wait_ge(s_bo, 16)
            normalise_b(0, 0)
            for t in range(GT):
                add_bias(0, t)
            with pool.Fori(0, GROUPS - 1) as g:
                group(g, False)
            group(GROUPS - 1, True)


def u_par(i):
    return i % 2


def moe_phase(nc, router_w, w1, w2, gate_up, down, gate_w, out, resid, ident, half_neg):
    ORDER = [0, 1, E, 2, 3, 4, 5, 6, 7]
    HIDDEN = len(ORDER)
    TURN = [0, 1, 2, 4, 5, 6, 7, 8, 9]
    TURNS = HIDDEN + 1
    BUFS = 3
    with ExitStack() as ctx:
        def sb(name, shape, dt=F32):
            return ctx.enter_context(nc.sbuf_tensor(name, shape, dt))

        def bank(name):
            return ctx.enter_context(nc.psum_tensor(name, [P, 512], F32))

        def sem(name):
            return ctx.enter_context(nc.semaphore(name))

        raw_up = sb("raw_up", [P, DC, E, F])
        raw_down = sb("raw_down", [P, FC, E, D])
        raw_gu = sb("raw_gu", [P, DC, 2 * F])
        raw_sd = sb("raw_sd", [P, FC, D])
        up_hi, up_lo = (sb(n, [P, DC, E, F], F32R) for n in ("up_hi", "up_lo"))
        dn_hi, dn_lo = (sb(n, [P, FC, E, D], F32R) for n in ("dn_hi", "dn_lo"))
        gu_hi, gu_lo = (sb(n, [P, DC, 2 * F], F32R) for n in ("gu_hi", "gu_lo"))
        sd_hi, sd_lo = (sb(n, [P, FC, D], F32R) for n in ("sd_hi", "sd_lo"))
        r_pad = sb("r_pad", [P, DC, P])
        r_hi, r_lo = (sb(n, [P, DC, P], F32R) for n in ("r_hi", "r_lo"))
        z = sb("z2", [P, GT, D])
        zT_hi, zT_lo = (sb(n, [P, DC, GR], F32R) for n in ("z2T_hi", "z2T_lo"))
        h_full = [sb(f"h_full{i}", [P, FC, GR]) for i in range(BUFS)]
        h_hi = [sb(f"h_hi{i}", [P, FC, GR], F32R) for i in range(BUFS)]
        h_lo = [sb(f"h_lo{i}", [P, FC, GR], F32R) for i in range(BUFS)]
        stats = sb("stats2", [P, GT, 6])
        mean_var = sb("mean_var2", [P, GT, 2])
        var_eps = sb("var_eps2", [P, GT])
        rstd = sb("rstd2", [P, GT])
        logitsT = sb("logitsT", [P, GR])
        logits = sb("logits", [P, GT, E + 1])
        nmax = sb("row_nmax", [P, GT])
        expo = sb("expo", [P, GT, E + 1])
        esum = sb("esum", [P, GT])
        einv = sb("einv", [P, GT])
        probs = sb("probs", [P, GT, E])
        top = sb("top", [P, GT, 8])
        top_at = sb("top_at", [P, GT, 8], U32)
        top_f = sb("top_f", [P, GT, 8])
        iota_u = sb("iota_u", [P, E], U32)
        iota = sb("iota", [P, E])
        chosen = sb("chosen", [P, GT, 2, E])
        gate_den = sb("gate_den", [P, GT, 1])
        combine = sb("combine", [P, GT, E + 1])
        up_ps = [bank(f"up_ps{k}") for k in range(4)]
        y_ps = [bank(f"y_ps{k}") for k in range(2)]
        r_ps = [bank(f"r_ps{k}") for k in range(2)]

        s_raw = [sem(f"layer{j}_in") for j in range(HIDDEN)]
        s_router_in, s_pad, s_iota = sem("router_in"), sem("router_padded"), sem("iota_ready")
        s_hi, s_lo = sem("weights_hi"), sem("weights_lo")
        s_st, s_mv, s_var, s_rstd, s_z = sem("row_stats"), sem("row_mean_var"), sem("row_var_eps"), sem("row_rstd"), sem("z2_ready")
        s_zt, s_zh, s_zl = sem("z2T_in_psum"), sem("z2T_hi_ready"), sem("z2T_lo_ready")
        s_lg, s_lgs, s_lt, s_lr = sem("logitsT_in_psum"), sem("logitsT_ready"), sem("logits_in_psum"), sem("logits_ready")
        s_nm, s_ex, s_chain = sem("row_max"), sem("row_exps"), sem("router_step")
        s_up, s_read, s_prod, s_hl = (sem("hidden_in_psum"), sem("hidden_read"), sem("gated_ready"), sem("h_lo_ready"))
        s_y, s_acc, s_out = sem("y_in_psum"), sem("y_added"), sem("out_stored")
        s_go, s_pgo = sem("vector_wait_met2"), sem("pool_wait_met2")
        FREE_U = 4

        parts = [(r_pad[:], r_hi[:], r_lo[:])]
        for e in ORDER:
            if e == E:
                parts += [(raw_gu[:], gu_hi[:], gu_lo[:]), (raw_sd[:], sd_hi[:], sd_lo[:])]
            else:
                parts += [(raw_up[:, :, e, :], up_hi[:, :, e, :], up_lo[:, :, e, :]),
                          (raw_down[:, :, e, :], dn_hi[:, :, e, :], dn_lo[:, :, e, :])]

        def tile(g, j, c):
            return FC * (TURNS * g + TURN[j]) + c

        def bank_of(turn, c):
            return up_ps[(turn % 2) * FC + c]

        block = ctx.enter_context(nc.Block())

        @block.sync
        def _(sp):
            sp.wait_ge(s_pad, 1)
            sp.dma_start(r_pad[:, :, 0:E], router_w.rearrange("(c p) e -> p c e", p=P)).then_inc(s_router_in, 16)
            sp.dma_start(r_pad[:, :, E:E + 1], gate_w.rearrange("(c p) e -> p c e", p=P), allow_slow_non_contiguous=True).then_inc(s_router_in, 16)
            for j, e in enumerate(ORDER):
                a, b = (gate_up, down) if e == E else (w1[e], w2[e])
                to = (raw_gu[:], raw_sd[:]) if e == E else (raw_up[:, :, e, :], raw_down[:, :, e, :])
                sp.dma_start(to[0], a.rearrange("(c p) f -> p c f", p=P)).then_inc(s_raw[j], 16)
                sp.dma_start(to[1], b.rearrange("(c p) d -> p c d", p=P)).then_inc(s_raw[j], 16)
            with sp.Fori(0, GROUPS) as g:
                sp.wait_ge(s_acc, 2 * HIDDEN * g + 2 * HIDDEN)
                rows = resid[:, bass.ds(GT * g, GT), :].rearrange("p (b h) d -> p b h d", h=2)
                sp.dma_start(out[bass.ds(2 * g, 2), 0:P - 1, :].rearrange("b p d -> p b d"),
                             rows[1:P, :, 0, :]).then_inc(s_out, 16)
                sp.dma_start(out[bass.ds(2 * g, 2), P - 1:N - 1, :].rearrange("b p d -> p b d"),
                             rows[:, :, 1, :]).then_inc(s_out, 16)
            sp.wait_ge(s_out, 32 * GROUPS)

        @block.tensor
        def _(pe):
            def transpose_z(g, first):
                pe.wait_ge(s_z, GT * g + GT)
                for c in range(DC):
                    if not first:
                        pe.wait_ge((s_lgs, s_lr)[c], g)
                    for t in range(GT):
                        m = pe.transpose(r_ps[c][:, t * P:(t + 1) * P], z[:, t, c * P:(c + 1) * P], ident[:])
                    m.then_inc(s_zt, 1)

            def router(g):
                for c in range(DC):
                    m = three(pe, r_ps[0][:], r_hi[:, c, :], r_lo[:, c, :], zT_hi[:, c, :], zT_lo[:, c, :],
                              c == 0, c == DC - 1)
                m.then_inc(s_lg, 1)

            def router_rows(g):
                pe.wait_ge(s_lgs, g + 1)
                for t in range(GT):
                    m = pe.transpose(r_ps[1][:, t * P:(t + 1) * P], logitsT[:, t * P:(t + 1) * P], ident[:])
                m.then_inc(s_lt, 1)

            def hidden(g, j):
                e = ORDER[j]
                for k in range(2 if e == E else 1):
                    for c2 in range(FC):
                        pe.wait_ge(s_read, tile(g, j, c2) + FC * k - 3 + FREE_U)
                        for c in range(DC):
                            if e == E:
                                cols = slice(k * F + c2 * P, k * F + (c2 + 1) * P)
                                w = gu_hi[:, c, cols], gu_lo[:, c, cols]
                            else:
                                cols = slice(c2 * P, (c2 + 1) * P)
                                w = up_hi[:, c, e, cols], up_lo[:, c, e, cols]
                            m = three(pe, bank_of(TURN[j] + k, c2)[:], *w, zT_hi[:, c, :], zT_lo[:, c, :],
                                      c == 0, c == DC - 1)
                        m.then_inc(s_up, 1)

            def down_rows(g, j, free):
                e, k = ORDER[j], j % BUFS
                pe.wait_ge(s_hl, HIDDEN * g + j + 1)
                for half in range(2):
                    if free:
                        pe.wait_ge(s_acc, 2 * (HIDDEN * g + j) - 1 + half)
                    for t in (2 * half, 2 * half + 1):
                        rows = slice(t * P, (t + 1) * P)
                        for c in range(FC):
                            w = (sd_hi[:, c, :], sd_lo[:, c, :]) if e == E else (dn_hi[:, c, e, :], dn_lo[:, c, e, :])
                            m = three(pe, y_ps[half][:, (t % 2) * D:(t % 2 + 1) * D], h_hi[k][:, c, rows],
                                      h_lo[k][:, c, rows], *w, c == 0, c == FC - 1)
                    m.then_inc(s_y, 1)

            def group(g, first, last):
                for j in range(1, HIDDEN):
                    if first:
                        pe.wait_ge(s_lo, 2 * j + 3)
                    hidden(g, j)
                    if j == 1:
                        router_rows(g)
                    down_rows(g, j - 1, not (first and j == 1))
                if not last:
                    transpose_z(g + 1, False)
                down_rows(g, HIDDEN - 1, True)
                if not last:
                    pe.wait_ge(s_zl, DC * (g + 2))
                    router(g + 1)
                    hidden(g + 1, 0)

            transpose_z(0, True)
            pe.wait_ge(s_zl, DC)
            pe.wait_ge(s_lo, 3)
            router(0)
            hidden(0, 0)
            group(0, True, False)
            with pe.Fori(1, GROUPS - 1) as g:
                group(g, False, False)
            group(GROUPS - 1, False, True)

        @block.scalar
        def _(act):
            act.sem_inc(s_read, FREE_U)

            def weights_hi(first, last):
                for n in range(first, last):
                    if n == 0:
                        act.wait_ge(s_router_in, 32)
                    else:
                        act.wait_ge(s_raw[(n - 1) // 2], 32)
                    act.activation(parts[n][1], parts[n][0], ACT.Copy).then_inc(s_hi, 1)

            def z_hi(g):
                for c in range(DC):
                    act.wait_ge(s_zt, DC * g + c + 1)
                    act.activation(zT_hi[:, c, :], r_ps[c][:], ACT.Copy).then_inc(s_zh, 1)

            def logits_copy(g):
                act.wait_ge(s_lg, g + 1)
                act.activation(logitsT[:], r_ps[0][:], ACT.Copy).then_inc(s_lgs, 1)

            def router_exps(g):
                act.wait_ge(s_nm, g + 1)
                for t in range(GT):
                    act.activation(expo[:, t, 0:E], logits[:, t, 0:E], ACT.Exp, bias=nmax[:, t:t + 1],
                                   accum_out=esum[:, t:t + 1])
                act.activation(expo[:, :, E:E + 1], logits[:, :, E:E + 1], ACT.Exp, scale=-1.0).then_inc(s_ex, 1)

            def hidden(g, j):
                e, k = ORDER[j], j % BUFS
                for c in range(FC):
                    n, src = tile(g, j, c), bank_of(TURN[j], c)
                    act.wait_ge(s_up, n + 1)
                    if e != E:
                        act.activation(h_hi[k][:, c, :], src[:], ACT.Silu)
                    act.activation(h_full[k][:, c, :], src[:], ACT.Silu).then_inc(s_read, 1)
                if e == E:
                    for c in range(FC):
                        act.wait_ge(s_prod, FC * g + c + 1)
                        act.activation(h_hi[k][:, c, :], h_full[k][:, c, :], ACT.Copy).then_inc(s_read, 1)

            def group(g, first, last):
                for j in range(1, HIDDEN):
                    if first and j + 1 < HIDDEN:
                        weights_hi(2 * j + 3, 2 * j + 5)
                    hidden(g, j)
                    if j == 1:
                        router_exps(g)
                if not last:
                    z_hi(g + 1)
                    logits_copy(g + 1)
                    hidden(g + 1, 0)

            weights_hi(0, 3)
            z_hi(0)
            logits_copy(0)
            hidden(0, 0)
            weights_hi(3, 5)
            group(0, True, False)
            with act.Fori(1, GROUPS - 1) as g:
                group(g, False, False)
            group(GROUPS - 1, False, True)

        @block.vector
        def _(dve):
            def weights_lo(first, last):
                for n in range(first, last):
                    dve.wait_ge(s_hi, n + 1)
                    dve.tensor_tensor(parts[n][2], parts[n][0], f32(parts[n][1]), ALU.subtract).then_inc(s_lo, 1)

            def layernorm_stats(g):
                for t in range(GT):
                    dve.bn_stats(stats[:, t, :], resid[:, GT * g + t, :]).then_inc(s_st, 1)
                for t in range(GT):
                    dve.wait_ge(s_st, GT * g + t + 1)
                    dve.sem_inc(s_go, 1)
                    dve.bn_aggr(mean_var[:, t, :], stats[:, t, :]).then_inc(s_mv, 1)

            def layernorm_apply(g):
                dve.wait_ge(s_rstd, g + 1)
                for t in range(GT):
                    dve.tensor_scalar(z[:, t, :], resid[:, GT * g + t, :], mean_var[:, t, 0:1], rstd[:, t:t + 1],
                                      ALU.subtract, ALU.mult).then_inc(s_z, 1)

            def z_lo(g):
                for c in range(DC):
                    dve.wait_ge(s_zh, DC * g + c + 1)
                    dve.tensor_tensor(zT_lo[:, c, :], r_ps[c][:], f32(zT_hi[:, c, :]), ALU.subtract).then_inc(s_zl, 1)

            def router(g):
                STEPS = 8
                step = [0]

                def done(ins):
                    step[0] += 1
                    ins.then_inc(s_chain, 1)
                    dve.wait_ge(s_chain, STEPS * g + step[0])
                    dve.sem_inc(s_go, 1)

                dve.wait_ge(s_lt, g + 1)
                dve.tensor_copy(logits[:], r_ps[1][:].rearrange("p (t e) -> p t e", t=GT)[:, :, 0:E + 1]).then_inc(s_lr, 1)
                dve.wait_ge(s_lr, g + 1)
                dve.tensor_reduce(nmax[:], logits[:, :, 0:E], AX_X, ALU.max, negate=True).then_inc(s_nm, 1)
                dve.wait_ge(s_ex, g + 1)
                dve.tensor_scalar(gate_den[:], expo[:, :, E:E + 1], 1.0, None, ALU.add)
                done(dve.reciprocal(einv[:], esum[:]))
                for t in range(GT):
                    m = dve.tensor_scalar(probs[:, t, :], expo[:, t, 0:E], einv[:, t:t + 1], None, ALU.mult)
                done(m)
                for t in range(GT):
                    m = dve.max(top[:, t, :], probs[:, t, :])
                done(m)
                for t in range(GT):
                    m = dve.max_index(top_at[:, t, :], top[:, t, :], probs[:, t, :])
                done(m)
                done(dve.tensor_copy(top_f[:], top_at[:]))
                for t in range(GT):
                    for n in range(2):
                        m = dve.scalar_tensor_tensor(out=chosen[:, t, n, :], in0=iota[:], scalar=top_f[:, t, n:n + 1],
                                                     in1=probs[:, t, :], op0=ALU.is_equal, op1=ALU.mult)
                done(m)
                done(dve.reciprocal(combine[:, :, E:E + 1], gate_den[:]))
                done(dve.tensor_tensor(combine[:, :, 0:E], chosen[:, :, 0, :], chosen[:, :, 1, :], ALU.add))

            def gate_product(g, j):
                k = j % BUFS
                for c in range(FC):
                    n = tile(g, j, c)
                    dve.wait_ge(s_read, n + 1 + FREE_U)
                    dve.wait_ge(s_up, n + FC + 1)
                    dve.tensor_tensor(h_full[k][:, c, :], bank_of(TURN[j] + 1, c)[:], h_full[k][:, c, :],
                                      ALU.mult).then_inc(s_prod, 1)

            def add_rows(g, j, first):
                e = ORDER[j]
                for half in range(2):
                    dve.wait_ge(s_y, 2 * (HIDDEN * g + j) + half + 1)
                    if not first:
                        dve.wait_ge(s_acc, 2 * (HIDDEN * g + j) - 1 + half)
                    for t in (2 * half, 2 * half + 1):
                        rows = resid[:, GT * g + t, :]
                        m = dve.scalar_tensor_tensor(out=rows, in0=y_ps[half][:, (t % 2) * D:(t % 2 + 1) * D],
                                                     scalar=combine[:, t, e:e + 1], in1=rows, op0=ALU.mult,
                                                     op1=ALU.add)
                    m.then_inc(s_acc, 1)

            def group(g, first, last):
                router(g)
                for j in range(1, HIDDEN):
                    if first and j + 1 < HIDDEN:
                        weights_lo(2 * j + 3, 2 * j + 5)
                    if ORDER[j] == E:
                        gate_product(g, j)
                    add_rows(g, j - 1, first and j == 1)
                    if not last and j == 4:
                        layernorm_stats(g + 1)
                    if not last and j == 6:
                        layernorm_apply(g + 1)
                if not last:
                    z_lo(g + 1)
                add_rows(g, HIDDEN - 1, False)

            layernorm_stats(0)
            layernorm_apply(0)
            weights_lo(0, 3)
            z_lo(0)
            dve.wait_ge(s_iota, 1)
            dve.tensor_copy(iota[:], iota_u[:])
            weights_lo(3, 5)
            group(0, True, False)
            with dve.Fori(1, GROUPS - 1) as g:
                group(g, False, False)
            group(GROUPS - 1, False, True)

        @block.gpsimd
        def _(pool):
            pool.memset(r_pad[:], 0.0).then_inc(s_pad, 1)
            pool.iota(iota_u[:], pattern=[[1, E]], base=0, channel_multiplier=0).then_inc(s_iota, 1)

            def layernorm_rstd(g):
                pool.wait_ge(s_mv, GT * g + GT)
                pool.sem_inc(s_pgo, 1)
                pool.tensor_scalar(var_eps[:], mean_var[:, :, 1], EPS_LN, None, ALU.add).then_inc(s_var, 1)
                pool.wait_ge(s_var, g + 1)
                pool.tensor_tensor(rstd[:], var_eps[:], half_neg[:], ALU.pow).then_inc(s_rstd, 1)

            def hidden_lo(g, j):
                k = j % BUFS
                for c in range(FC):
                    n = tile(g, j, c) + (FC if ORDER[j] == E else 0)
                    pool.wait_ge(s_read, n + 1 + FREE_U)
                    m = pool.tensor_tensor(h_lo[k][:, c, :], h_full[k][:, c, :], f32(h_hi[k][:, c, :]), ALU.subtract)
                m.then_inc(s_hl, 1)

            def group(g, last):
                for j in range(1, HIDDEN):
                    hidden_lo(g, j)
                    if j == 4 and not last:
                        layernorm_rstd(g + 1)
                if not last:
                    hidden_lo(g + 1, 0)

            layernorm_rstd(0)
            hidden_lo(0, 0)
            with pool.Fori(0, GROUPS - 1) as g:
                group(g, False)
            group(GROUPS - 1, True)


_INS = ["x", "L0_tok_W", "L0_tok_b", "L0_attn_Wq", "L0_attn_Wk", "L0_attn_Wv", "L0_attn_Wo", "L0_attn_bo",
        "L0_ffn_router_w", "L0_ffn_w1", "L0_ffn_w2", "L0_ffn_shared_gate_up", "L0_ffn_shared_down",
        "L0_ffn_shared_gate_w"]
_OUT = ((B, N - 1, D), "float32")


def kernel(**inputs):
    import numpy as _np
    import concourse.bacc as _bacc
    from concourse import mybir as _mybir
    from concourse.bass_utils import run_bass_kernel_spmd as _run

    nc = _bacc.Bacc("TRN2", target_bir_lowering=False, num_devices=1)
    arrays, args = {}, []
    for name in _INS:
        a = _np.ascontiguousarray(inputs[name])
        arrays[f"in_{name}_dram"] = a
        args.append(nc.dram_tensor(f"in_{name}_dram", a.shape, _mybir.dt.from_np(a.dtype), kind="ExternalInput").ap())
    out = nc.dram_tensor("out_0_dram", _OUT[0], _mybir.dt.from_np(_np.dtype(_OUT[1])), kind="ExternalOutput").ap()
    build(nc, *args, out)
    r = _run(nc, [arrays], core_ids=[0])
    return r.results[0]["out_0_dram"]
```

```python
from contextlib import ExitStack

import concourse.bass as bass
from concourse import mybir

P = 128
B, N, D = 16, 256, 256
DC = D // P
HEADS, DH = 16, 64
INNER = HEADS * DH
PAIRS = HEADS // 2
GROUPS = B // 2
GT = 4
GR = GT * P
E, F = 8, 256
FC = F // P
UNITS = 2 * PAIRS
SCALE = DH ** -0.5
EPS_LN, EPS_SM = 1e-5, 1e-10
ROWS = B * N
TOP = 2
SHIFT = 7
HALF = 6
BITS = 3
CAP = ROWS + P
TILES = -(-(TOP * ROWS // P + E - 1) // (2 * HALF)) * 2 * HALF

ALU = mybir.AluOpType
ACT = mybir.ActivationFunctionType
F32 = mybir.dt.float32
F32R = mybir.dt.float32r
BF16 = mybir.dt.bfloat16
U32 = mybir.dt.uint32
AX_X = mybir.AxisListType.X


def f32(ap):
    return ap.bitcast(F32)


def three(pe, out, wh, wl, xh, xl, start, stop):
    pe.matmul(out, wl, xh, start=start, stop=False, skip_group_check=True)
    pe.matmul(out, wh, xl, start=False, stop=False, skip_group_check=True)
    return pe.matmul(out, wh, xh, start=False, stop=stop, skip_group_check=True)


def build(nc, x, tok_w, tok_b, wq, wk, wv, wo, bo, router_w, w1, w2, gate_up, down, gate_w, out):
    x_rows = x.rearrange("b (h p) d -> p (b h) d", p=P)
    with ExitStack() as ctx:
        resid = ctx.enter_context(nc.sbuf_tensor("resid", [P, B * N // P, D], F32))
        ident = ctx.enter_context(nc.sbuf_tensor("ident", [P, P], F32))
        half_neg = ctx.enter_context(nc.sbuf_tensor("half_neg", [P, GT], F32))
        slots = ctx.enter_context(nc.sbuf_tensor("slots", [P, B * N // P, TOP], U32))
        shares = ctx.enter_context(nc.sbuf_tensor("shares", [P, B * N // P, TOP + 1], F32))
        tile_expert = ctx.enter_context(nc.sbuf_tensor("tile_expert", [1, TILES // HALF], U32))
        tile_in = ctx.enter_context(nc.sbuf_tensor("tile_in", [1, TILES], U32))
        z_dram = nc.dram_tensor("z_rows", (GROUPS, P, GT, D), F32).ap()
        x_slots = nc.dram_tensor("expert_in_rows", (E * CAP + P, D), F32).ap()
        y_slots = nc.dram_tensor("expert_out_rows", (TILES * P, D), F32).ap()
        with ExitStack() as weights:
            qkv_parts = [weights.enter_context(nc.sbuf_tensor(n, [P, DC, INNER], F32R))
                         for n in ("wq_hi", "wq_lo", "wk_hi", "wk_lo", "wv_hi", "wv_lo")]
            wo_parts = [weights.enter_context(nc.sbuf_tensor(n, [P, PAIRS, D], F32R))
                        for n in ("wo_hi", "wo_lo")]
            token_phase(nc, x, x_rows, tok_w, tok_b, wq, wk, wv, wo, resid, ident, half_neg,
                        qkv_parts, wo_parts)
            attention_phase(nc, bo, router_w, gate_w, resid, ident, half_neg, qkv_parts, wo_parts,
                            slots, shares, (tile_expert, tile_in), z_dram, x_slots)
        expert_phase(nc, w1, w2, gate_up, down, out, resid, ident, slots, shares,
                     (tile_expert, tile_in), z_dram, x_slots, y_slots)


def token_phase(nc, x, x_rows, tok_w, tok_b, wq, wk, wv, wo, resid, ident, half_neg,
                qkv_parts, wo_parts):
    with ExitStack() as ctx:
        def sb(name, shape, dt=F32):
            return ctx.enter_context(nc.sbuf_tensor(name, shape, dt))

        def sem(name):
            return ctx.enter_context(nc.semaphore(name))

        xin = [sb(f"xin{i}", [P, GT, D]) for i in range(2)]
        xT_hi, xT_lo = (sb(n, [P, DC, GR], F32R) for n in ("xT_hi", "xT_lo"))
        hT = sb("hT", [P, DC, GR])
        raw = [sb(f"raw_{n}", [P, INNER // P, D]) for n in "qkv"]
        raw_o = sb("raw_o", [P, DC, INNER])
        tokw = sb("tokw", [P, 2 * DC, D])
        tokw_hi, tokw_lo = (sb(n, [P, DC, D], F32R) for n in ("tokw_hi", "tokw_lo"))
        ro = sb("ro", [B, D])
        roT = sb("roT", [P, DC, B])
        bcol = sb("bcol", [P, DC])
        rbias = sb("rbias", [P, DC, B])
        xT_ps = [ctx.enter_context(nc.psum_tensor(f"xT_ps{c}", [P, 512], F32)) for c in range(2)]
        tok_ps = [ctx.enter_context(nc.psum_tensor(f"tok_ps{c}", [P, 512], F32)) for c in range(2)]
        h_ps = [ctx.enter_context(nc.psum_tensor(f"h_ps{c}", [P, 512], F32)) for c in range(2)]
        w_ps = [ctx.enter_context(nc.psum_tensor(f"w_ps{c}", [P, 512], F32)) for c in range(2)]

        x_in = [sem(f"x_in{i}") for i in range(2)]
        s_ro, s_tokw, s_bcol = sem("ro_in"), sem("tokw_in"), sem("bcol_in")
        s_raw = [sem(f"raw_in{i}") for i in range(4)]
        s_zero, s_ident, s_half = sem("ident_zeroed"), sem("ident_ready"), sem("half_ready")
        s_roT_ps, s_roT, s_r_ps, s_rbias = sem("roT_ps"), sem("roT_ready"), sem("r_ps"), sem("rbias")
        s_tw_hi, s_tw_lo = sem("tokw_hi_ready"), sem("tokw_lo_ready")
        s_xT_ps, s_xT_hi, s_xT_lo = sem("xT_in_psum"), sem("xT_hi_ready"), sem("xT_lo_ready")
        s_tok, s_gelu = sem("tok_in_psum"), sem("hT_ready")
        s_h, s_res = sem("h_in_psum"), sem("resid_written")
        s_w, s_w_hi, s_w_lo = sem("w_in_psum"), sem("w_hi_ready"), sem("w_lo_ready")

        banks = []
        for w in range(3):
            for c in range(DC):
                for half in range(2):
                    src = [(raw[w][:, 4 * half + r, c * P:(c + 1) * P]) for r in range(4)]
                    dst = [qkv_parts[2 * w + k][:, c, 512 * half:512 * half + 512] for k in range(2)]
                    banks.append((w, src, dst, SCALE if w == 0 else 1.0))
        for pp in range(0, PAIRS, 2):
            src = [raw_o[:, c, (pp + i) * P:(pp + i + 1) * P] for i in range(2) for c in range(DC)]
            dst = [wo_parts[k][:, pp:pp + 2, :] for k in range(2)]
            banks.append((3, src, dst, 1.0))
        per_group = len(banks) // GROUPS

        block = ctx.enter_context(nc.Block())

        @block.sync
        def _(sp):
            sp.dma_start(ro[:], x[:, 0, :]).then_inc(s_ro, 16)
            sp.dma_start(tokw[:], tok_w.rearrange("(c p) e -> p c e", p=P)).then_inc(s_tokw, 16)
            sp.dma_start(xin[0][:], x_rows[:, 0:GT, :]).then_inc(x_in[0], 16)
            sp.dma_start(xin[1][:], x_rows[:, GT:2 * GT, :]).then_inc(x_in[1], 16)
            for i, w in enumerate((wq, wk, wv)):
                sp.dma_start(raw[i][:], w.rearrange("(r p) d -> p r d", p=P)).then_inc(s_raw[i], 16)
            sp.dma_start(raw_o[:], wo.rearrange("(c p) i -> p c i", p=P)).then_inc(s_raw[3], 16)
            for g in range(2, GROUPS):
                sp.wait_ge(s_xT_ps, DC * (g - 1))
                sp.dma_start(xin[g % 2][:], x_rows[:, GT * g:GT * g + GT, :]).then_inc(x_in[g % 2], 16)

        @block.gpsimd
        def _(pool):
            pool.memset(ident[:], 0.0).then_inc(s_zero, 1)
            pool.memset(half_neg[:], -0.5).then_inc(s_half, 1)
            pool.wait_ge(s_zero, 1)
            pool.affine_select(out=ident[:], in_=ident[:], compare_op=ALU.not_equal, fill=1.0, base=0,
                               pattern=[[-1, P]], channel_multiplier=1).then_inc(s_ident, 1)

        def transpose_x(pe, g):
            k = g % 2
            pe.wait_ge(x_in[k], 16 * (g // 2 + 1))
            for c in range(DC):
                for t in range(GT):
                    m = pe.transpose(xT_ps[c][:, t * P:(t + 1) * P], xin[k][:, t, c * P:(c + 1) * P], ident[:])
                m.then_inc(s_xT_ps, 1)

        @block.tensor
        def _(pe):
            pe.wait_ge(s_ident, 1)
            pe.wait_ge(s_ro, 16)
            for c in range(DC):
                m = pe.transpose(h_ps[0][:, c * B:(c + 1) * B], ro[:, c * P:(c + 1) * P], ident[:B, :B])
            m.then_inc(s_roT_ps, 1)
            transpose_x(pe, 0)
            pe.wait_ge(s_roT, 1)
            pe.wait_ge(s_tokw, 16)
            for e in range(DC):
                for c in range(DC):
                    m = pe.matmul(h_ps[1][:, e * B:(e + 1) * B], tokw[:, DC + c, e * P:(e + 1) * P], roT[:, c, :],
                                  start=c == 0, stop=c == DC - 1)
            m.then_inc(s_r_ps, 1)

            def group(g, last):
                pe.wait_ge(s_xT_lo, DC * g + DC)
                if g == 0:
                    pe.wait_ge(s_tw_lo, 1)
                else:
                    pe.wait_ge(s_gelu, 4 * g)
                for e in range(DC):
                    for c in range(DC):
                        m = three(pe, tok_ps[e][:], tokw_hi[:, c, e * P:(e + 1) * P],
                                  tokw_lo[:, c, e * P:(e + 1) * P], xT_hi[:, c, :], xT_lo[:, c, :],
                                  c == 0, c == DC - 1)
                    m.then_inc(s_tok, 1)
                if not last:
                    transpose_x(pe, g + 1)

            def weights(g):
                for j in range(per_group):
                    n = per_group * g + j
                    which, src, _, _ = banks[n]
                    pe.wait_ge(s_raw[which], 16)
                    if n >= 2:
                        pe.wait_ge(s_w_lo, n - 1)
                    for i, s in enumerate(src):
                        m = pe.transpose(w_ps[j][:, i * P:(i + 1) * P], s, ident[:])
                    m.then_inc(s_w, 1)

            def rows(g):
                pe.wait_ge(s_gelu, 4 * g + 4)
                if g == 0:
                    pe.wait_ge(s_rbias, 1)
                else:
                    pe.wait_ge(s_res, 2 * g)
                for j in range(2):
                    for t in range(2):
                        for c in range(DC):
                            o = t * D + c * P
                            m = pe.transpose(h_ps[j][:, o:o + P], hT[:, c, (2 * j + t) * P:(2 * j + t + 1) * P], ident[:])
                    m.then_inc(s_h, 1)

            for g in range(GROUPS):
                group(g, g == GROUPS - 1)
                weights(g)
                rows(g)

        @block.scalar
        def _(act):
            act.dma_start(bcol[:], tok_b.rearrange("(c p) -> p c", p=P), allow_slow_non_contiguous=True).then_inc(s_bcol, 16)
            act.wait_ge(s_tokw, 16)
            act.activation(tokw_hi[:], tokw[:, 0:DC, :], ACT.Copy).then_inc(s_tw_hi, 1)

            def x_hi(g):
                for c in range(DC):
                    act.wait_ge(s_xT_ps, DC * g + c + 1)
                    if g:
                        act.wait_ge(s_tok, DC * g)
                    act.activation(xT_hi[:, c, :], xT_ps[c][:], ACT.Copy).then_inc(s_xT_hi, 1)

            x_hi(0)
            for g in range(GROUPS):
                if g + 1 < GROUPS:
                    x_hi(g + 1)
                if g == 0:
                    act.wait_ge(s_rbias, 1)
                for e in range(DC):
                    act.wait_ge(s_tok, DC * g + e + 1)
                    if g and e == 0:
                        act.wait_ge(s_h, 2 * g)
                    for b in range(2):
                        n = 2 * g + b
                        act.activation(hT[:, e, b * N:(b + 1) * N], tok_ps[e][:, b * N:(b + 1) * N], ACT.Gelu,
                                       bias=rbias[:, e, n:n + 1]).then_inc(s_gelu, 1)
                for j in range(per_group):
                    n = per_group * g + j
                    act.wait_ge(s_w, n + 1)
                    hi = banks[n][2][0]
                    src = w_ps[j][:] if banks[n][0] < 3 else w_ps[j][:].rearrange("p (i d) -> p i d", i=2)
                    act.activation(hi, src, ACT.Copy, scale=banks[n][3]).then_inc(s_w_hi, 1)

        @block.vector
        def _(dve):
            dve.wait_ge(s_roT_ps, 1)
            dve.tensor_copy(roT[:], h_ps[0][:, 0:DC * B].rearrange("p (c b) -> p c b", c=DC)).then_inc(s_roT, 1)
            dve.wait_ge(s_tw_hi, 1)
            dve.tensor_tensor(tokw_lo[:], tokw[:, 0:DC, :], f32(tokw_hi[:]), ALU.subtract).then_inc(s_tw_lo, 1)
            dve.wait_ge(s_r_ps, 1)
            dve.wait_ge(s_bcol, 16)
            for e in range(DC):
                m = dve.tensor_scalar(rbias[:, e, :], h_ps[1][:, e * B:(e + 1) * B], bcol[:, e:e + 1], None, ALU.add)
            m.then_inc(s_rbias, 1)

            def x_lo(g):
                for c in range(DC):
                    dve.wait_ge(s_xT_hi, DC * g + c + 1)
                    dve.tensor_tensor(xT_lo[:, c, :], xT_ps[c][:], f32(xT_hi[:, c, :]), ALU.subtract).then_inc(s_xT_lo, 1)

            x_lo(0)
            for g in range(GROUPS):
                if g + 1 < GROUPS:
                    x_lo(g + 1)
                for j in range(per_group):
                    n = per_group * g + j
                    dve.wait_ge(s_w_hi, n + 1)
                    hi, lo = banks[n][2]
                    src = w_ps[j][:] if banks[n][0] < 3 else w_ps[j][:].rearrange("p (i d) -> p i d", i=2)
                    dve.scalar_tensor_tensor(out=lo, in0=src, scalar=banks[n][3], in1=f32(hi), op0=ALU.mult,
                                             op1=ALU.subtract).then_inc(s_w_lo, 1)
                for j in range(2):
                    dve.wait_ge(s_h, 2 * g + j + 1)
                    dve.tensor_copy(resid[:, GT * g + 2 * j:GT * g + 2 * j + 2, :],
                                    h_ps[j][:].rearrange("p (t d) -> p t d", t=2)).then_inc(s_res, 1)


def attention_phase(nc, bo, router_w, gate_w, resid, ident, half_neg, qkv_parts, wo_parts, slots, shares,
                    tile_tables, z_dram, x_slots):
    tile_expert, tile_in = tile_tables
    wq_hi, wq_lo, wk_hi, wk_lo, wv_hi, wv_lo = qkv_parts
    wo_hi, wo_lo = wo_parts
    with ExitStack() as ctx:
        def sb(name, shape, dt=F32):
            return ctx.enter_context(nc.sbuf_tensor(name, shape, dt))

        def bank(name):
            return ctx.enter_context(nc.psum_tensor(name, [P, 512], F32))

        def sem(name):
            return ctx.enter_context(nc.semaphore(name))

        bo_row = sb("bo_row", [P, D])
        z = sb("z", [P, GT, D])
        zT_hi, zT_lo = (sb(n, [P, DC, GR], F32R) for n in ("zT_hi", "zT_lo"))
        qk = [[[sb(f"{n}_{part}{i}", [P, GR], F32R) for part in ("hi", "lo")] for n in "qk"] for i in range(2)]
        v = [sb(f"v{i}", [P, GT, 2 * P]) for i in range(2)]
        prob = [sb(f"prob{i}", [P, 2, 2, N]) for i in range(2)]
        probT = [sb(f"probT{i}", [P, 2, 2, N]) for i in range(2)]
        oT_hi, oT_lo = (sb(n, [P, PAIRS, GR], F32R) for n in ("oT_hi", "oT_lo"))
        nmax = [sb(f"nmax{i}", [P, 4]) for i in range(2)]
        rsum = [sb(f"rsum{i}", [P, 4]) for i in range(2)]
        rsum_eps = sb("rsum_eps", [P, 4])
        rinv = [sb(f"rinv{i}", [P, 4]) for i in range(2)]
        stats = sb("stats", [P, GT, 6])
        mean_var = sb("mean_var", [P, GT, 2])
        var_eps = sb("var_eps", [P, GT])
        rstd = sb("rstd", [P, GT])
        stats2, mean_var2 = sb("stats2", [P, GT, 6]), sb("mean_var2", [P, GT, 2])
        var_eps2, rstd2 = sb("var_eps2", [P, GT]), sb("rstd2", [P, GT])
        s_ps = [bank(f"s_ps{h}") for h in range(2)]
        pT_ps = [bank(f"pT_ps{h}") for h in range(2)]
        o_ps = bank("o_ps")
        proj_ps = [bank(f"proj_ps{j}") for j in range(2)]
        v_ps = bank("v_ps")

        r_pad = sb("r_pad", [P, DC, P])
        r_hi, r_lo = (sb(n, [P, DC, P], F32R) for n in ("r_hi", "r_lo"))
        z2 = sb("z2", [P, GT, D])
        z2T_hi, z2T_lo = (sb(n, [P, DC, GR], F32R) for n in ("z2T_hi", "z2T_lo"))
        logitsT = sb("logitsT", [P, GR])
        logits = sb("logits", [P, GT, E + 1])
        row_nmax = sb("row_nmax", [P, GT])
        expo = sb("expo", [P, GT, E + 1])
        esum = sb("esum", [P, GT])
        einv = sb("einv", [P, GT])
        gate_den = sb("gate_den", [P, GT, 1])
        probs = sb("probs", [P, GT, E])
        top = sb("top", [P, GT, 8])
        top_at = sb("top_at", [P, GT, 8], U32)
        top_f = sb("top_f", [P, GT, 8])
        hot = sb("hot", [P, TOP, GT, E])
        taken = sb("taken", [P, GT, E], BF16)
        before = sb("before", [P, P], BF16)
        ones = sb("ones", [P, P], BF16)
        run = sb("run", [P, GT + 1, E])
        ranks = sb("ranks", [P, 2, GT, E])
        place = sb("place", [P, GT, E])
        picked = sb("picked", [P, TOP, GT, E])
        slot_f = sb("slot_f", [P, GT, TOP])
        slot_now = sb("slot_now", [P, GT, TOP], U32)
        slots_in = sb("slots_in", [P, B * N // P, TOP])
        skipped = sb("skipped", [P, B * N // P * TOP])
        passed = (probT[0][:].rearrange("p a b c -> p (a b c)")[:, 0:(E - 1) * (B * N // P) * TOP]
                  .rearrange("p (e n) -> p e n", e=E - 1))
        iota_u = sb("iota_u", [P, E], U32)
        iota = sb("iota", [P, E])
        fill = sb("fill", [1, E], U32)
        tiles_u = sb("tiles_u", [P, E], U32)
        tiles_f = sb("tiles_f", [P, E])
        ends = sb("ends", [1, E])
        skips = sb("skips", [P, E])
        turn_u = sb("turn_u", [1, TILES + HALF], U32)
        turn_f = sb("turn_f", [1, TILES + HALF])
        place_value = sb("place_value", [1, TILES // HALF, HALF])
        words = sb("words", [1, TILES // HALF])
        past, past_rows = (v[i][0:1].rearrange("a t d -> a (t d)")[:, 0:E * (TILES + HALF)].rearrange("a (e t) -> a e t", e=E)
                           for i in range(2))
        table_e = sb("table_e", [1, TILES + HALF])
        table_r = sb("table_r", [1, TILES + HALF])
        rows_f = sb("rows_f", [1, TILES + HALF])

        s_bo = sem("bo_in")
        s_r_zero, s_r_in, s_r_hi, s_r_lo = sem("router_padded"), sem("router_in"), sem("r_hi_ready"), sem("r_lo_ready")
        s_iotas, s_consts = sem("iotas"), sem("router_constants")
        s_before0 = sem("before_set")
        s_st2, s_mv2, s_var2, s_rstd2, s_z2 = (sem("row_stats"), sem("row_mean_var"), sem("row_var_eps"),
                                               sem("row_rstd"), sem("z2_ready"))
        s_zt2, s_zh2, s_zl2 = sem("z2T_in_psum"), sem("z2T_hi_ready"), sem("z2T_lo_ready")
        s_lg, s_lgs, s_lt, s_lr = sem("logitsT_in_psum"), sem("logitsT_ready"), sem("logits_in_psum"), sem("logits_ready")
        s_nm, s_ex, s_chain, s_chain2 = sem("row_max"), sem("row_exps"), sem("router_step"), sem("place_step")
        s_taken, s_rank, s_rank_read, s_slot = sem("taken_ready"), sem("ranks_in_psum"), sem("ranks_read"), sem("slots_ready")
        s_scat, s_zst, s_z2_free, s_tail, s_table = sem("rows_scattered"), sem("z_stored"), sem("z2_free"), sem("fill_ready"), sem("table_step")
        s_fill, s_placed = sem("fill_stored"), sem("places_ready")
        s_mask = sem("masked_key_zeroed")
        s_S, s_max, s_exp = sem("scores"), sem("neg_max"), sem("exps")
        s_sum, s_rinv, s_nA, s_nB = sem("sum_eps"), sem("sum_inverse"), sem("normal_A"), sem("normal_B")
        s_T, s_pA, s_pB = sem("transposed"), sem("probT_A"), sem("probT_B")
        s_o, s_oh, s_ol = sem("o_in_psum"), sem("oT_hi_ready"), sem("oT_lo_ready")
        s_qk, s_qkh, s_qkl = sem("qk_in_psum"), sem("qk_hi_ready"), sem("qk_lo_ready")
        s_v, s_ve = sem("v_in_psum"), sem("v_ready")
        s_zt, s_zh, s_zl = sem("zT_in_psum"), sem("zT_hi2"), sem("zT_lo2")
        s_st, s_mv, s_var, s_rstd, s_z, s_bias = (sem("bn_stats"), sem("mean_var"), sem("var_eps"), sem("rstd"),
                                                  sem("z_ready"), sem("bo_added"))
        s_wo, s_woe = sem("out_rows_in_psum"), sem("out_rows_added")
        s_go, s_pgo = sem("vector_wait_met"), sem("pool_wait_met")

        FREE_P = 4
        FREE_B = 1
        FREE_W = 2

        CHOICE_STEPS, PLACE_STEPS = 6, GT + 3

        def fill_up(eng, experts):
            eng.wait_ge(s_tail, 1)
            for e in experts:
                at = eng.value_load(fill[0:1, e:e + 1], min_val=e * CAP, max_val=e * CAP + ROWS)
                eng.dma_start(x_slots[bass.ds(at, P), :], z2[:, 0, :]).then_inc(s_fill, 16)

        block = ctx.enter_context(nc.Block())

        @block.sync
        def _(sp):
            sp.dma_start(bo_row[:], bo.rearrange("(a d) -> a d", a=1).broadcast_to([P, D])).then_inc(s_bo, 16)
            sp.wait_ge(s_r_zero, 1)
            sp.dma_start(r_pad[:, :, 0:E], router_w.rearrange("(c p) e -> p c e", p=P)).then_inc(s_r_in, 16)
            sp.dma_start(r_pad[:, :, E:E + 1], gate_w.rearrange("(c p) e -> p c e", p=P),
                         allow_slow_non_contiguous=True).then_inc(s_r_in, 16)
            sp.sem_inc(s_z2_free, 1)
            with sp.Fori(0, GROUPS - 1) as r:
                sp.wait_ge(s_z2, GT * r + GT)
                sp.dma_start(z_dram[bass.ds(r, 1)].rearrange("a p t d -> p (a t) d"), z2[:]).then_inc(s_zst, 16)
                sp.wait_ge(s_zst, 16 * r + 16)
                sp.wait_ge(s_scat, 16 * GT * TOP * (r + 1))
                sp.sem_inc(s_z2_free, 1)
            sp.wait_ge(s_z2, GT * GROUPS)
            sp.dma_start(z_dram[GROUPS - 1], z2[:]).then_inc(s_zst, 16)
            fill_up(sp, range(0, E, 2))
            sp.dma_start(x_slots[E * CAP:E * CAP + P, :], z2[:, 0, :]).then_inc(s_fill, 16)
            sp.wait_ge(s_zst, 16 * GROUPS)
            sp.wait_ge(s_fill, 16 * (E + 1))


        @block.tensor
        def _(pe):
            pe.sem_inc(s_T, FREE_P)

            def transpose_z(g, free):
                pe.wait_ge(s_z, GT * g + GT)
                for c in range(DC):
                    if free:
                        pe.wait_ge(s_qkl, UNITS * g - 1 + c)
                    for t in range(GT):
                        m = pe.transpose(proj_ps[c][:, t * P:(t + 1) * P], z[:, t, c * P:(c + 1) * P], ident[:])
                    m.then_inc(s_zt, 1)

            def project_qk(g, j):
                hi, lo = (wq_hi, wq_lo) if j % 2 == 0 else (wk_hi, wk_lo)
                cols = slice((j // 2) * P, (j // 2 + 1) * P)
                for c in range(DC):
                    m = three(pe, proj_ps[j % 2][:], hi[:, c, cols], lo[:, c, cols], zT_hi[:, c, :], zT_lo[:, c, :],
                              c == 0, c == DC - 1)
                m.then_inc(s_qk, 1)

            def project_v(g, j):
                t, cols = j % 4, slice((j // 4) * 2 * P, (j // 4 + 1) * 2 * P)
                rows = slice(t * P, (t + 1) * P)
                for c in range(DC):
                    m = three(pe, v_ps[:, 0:2 * P], zT_hi[:, c, rows], zT_lo[:, c, rows], wv_hi[:, c, cols],
                              wv_lo[:, c, cols], c == 0, c == DC - 1)
                m.then_inc(s_v, 1)

            def scores(g, i, free):
                u, pair, b = UNITS * g + i, i // 2, i % 2
                (q_hi, q_lo), (k_hi, k_lo) = qk[pair % 2]
                pe.wait_ge(s_qkl, UNITS * g + 2 * pair + 2)
                if free:
                    pe.wait_ge(s_exp, 2 * u)
                keys = slice(b * N, (b + 1) * N)
                for qt in range(2):
                    rows = slice(b * N + qt * P, b * N + (qt + 1) * P)
                    for n, (a, k) in enumerate(((q_lo, k_hi), (q_hi, k_lo), (q_hi, k_hi))):
                        for h in range(2):
                            part = slice(h * DH, (h + 1) * DH)
                            m = pe.matmul(s_ps[h][:, qt * N:(qt + 1) * N], a[part, rows], k[part, keys],
                                          start=n == 0, stop=n == 2)
                            if qt == 1 and n == 2:
                                m.then_inc(s_S, 1)

            def transpose_p(g, i):
                u = UNITS * g + i
                for h, (normal, free) in enumerate(((s_nA, s_pA), (s_nB, s_pB))):
                    pe.wait_ge(normal, u + 1)
                    pe.wait_ge(free, u + FREE_B)
                    for kt in range(2):
                        for qt in range(2):
                            o = kt * N + qt * P
                            m = pe.transpose(pT_ps[h][:, o:o + P], prob[u_par(i)][:, h, qt, kt * P:(kt + 1) * P], ident[:])
                    m.then_inc(s_T, 1)

            def values(g, i):
                u, pair, b = UNITS * g + i, i // 2, i % 2
                pe.wait_ge(s_ve, UNITS * g + 4 * (pair // 2) + 4)
                pe.wait_ge(s_ol, u + FREE_B)
                pe.wait_ge(s_pA, u + 1 + FREE_B)
                pe.wait_ge(s_pB, u + 1 + FREE_B)
                vt = v[(pair // 2) % 2]
                for kt in range(2):
                    for h in range(2):
                        col = (pair % 2) * P + h * DH
                        m = pe.matmul(o_ps[h * DH:(h + 1) * DH, 0:N], vt[:, 2 * b + kt, col:col + DH],
                                      probT[u_par(i)][:, h, kt, :], start=kt == 0, stop=kt == 1)
                m.then_inc(s_o, 1)

            def output_rows(g, last):
                for j in range(2):
                    pe.wait_ge(s_ol, UNITS * g + UNITS - 1 + j + FREE_B)
                    pe.wait_ge(s_qkl, UNITS * g + UNITS + (-1 if last else 3) + j)
                    for t in (2 * j, 2 * j + 1):
                        rows = slice(t * P, (t + 1) * P)
                        for pair in range(PAIRS):
                            m = three(pe, proj_ps[j][:, (t % 2) * D:(t % 2 + 1) * D], oT_hi[:, pair, rows],
                                      oT_lo[:, pair, rows], wo_hi[:, pair, :], wo_lo[:, pair, :],
                                      pair == 0, pair == PAIRS - 1)
                    m.then_inc(s_wo, 1)

            def router_step(g, i):
                r, ps = g - 1, proj_ps[(i + 1) % 2]
                if i in (3, 4):
                    c = i - 3
                    if c == 0:
                        pe.wait_ge(s_z2, GT * r + GT)
                    idle_bank(g, i)
                    for t in range(GT):
                        m = pe.transpose(ps[:, t * P:(t + 1) * P], z2[:, t, c * P:(c + 1) * P], ident[:])
                    m.then_inc(s_zt2, 1)
                elif i == 5:
                    pe.wait_ge(s_zl2, DC * r + DC)
                    idle_bank(g, i)
                    for c in range(DC):
                        m = three(pe, ps[:], r_hi[:, c, :], r_lo[:, c, :], z2T_hi[:, c, :], z2T_lo[:, c, :],
                                  c == 0, c == DC - 1)
                    m.then_inc(s_lg, 1)
                elif i == 6:
                    pe.wait_ge(s_lgs, r + 1)
                    idle_bank(g, i)
                    for t in range(GT):
                        m = pe.transpose(ps[:, t * P:(t + 1) * P], logitsT[:, t * P:(t + 1) * P], ident[:])
                    m.then_inc(s_lt, 1)
                elif i == 10:
                    pe.wait_ge(s_taken, r + 1)
                    idle_bank(g, i)
                    pe.matmul(ps[:, 0:GT * E], before[:], taken[:].rearrange("p t e -> p (t e)"), start=True, stop=True)
                    pe.matmul(ps[:, GT * E:2 * GT * E], ones[:], taken[:].rearrange("p t e -> p (t e)"),
                              start=True, stop=True).then_inc(s_rank, 1)

            def idle_bank(g, i):
                if g is not GROUPS:
                    pe.wait_ge(s_qkl, UNITS * g + i + 4)

            def router_bank_read(g, i):
                r = g - 1
                if i in (4, 5):
                    pe.wait_ge(s_zl2, DC * r + i - 3)
                elif i == 6:
                    pe.wait_ge(s_lgs, r + 1)
                elif i == 7:
                    pe.wait_ge(s_lr, r + 1)
                elif i == 11:
                    pe.wait_ge(s_rank_read, r + 1)

            def group(g, first, last):
                for i in range(UNITS):
                    ahead = i + 4
                    if i == UNITS - 4 and not last:
                        transpose_z(g + 1, True)
                    if i + 1 < UNITS:
                        scores(g, i + 1, True)
                    elif not last:
                        scores(g + 1, 0, True)

                    def next_qk():
                        if ahead >= UNITS and last:
                            return
                        if not first:
                            router_bank_read(g, i)
                        if i < 2:
                            pe.wait_ge(s_woe, 2 * g + i - 1 + FREE_W)
                        pe.wait_ge(s_qkl, UNITS * g + ahead - 1)
                        project_qk(g + ahead // UNITS, ahead % UNITS)

                    def next_v():
                        if ahead < UNITS or not last:
                            pe.wait_ge(s_ve, UNITS * g + ahead)
                            if i == UNITS - 4:
                                pe.wait_ge(s_zl, DC * (g + 2))
                            project_v(g + ahead // UNITS, ahead % UNITS)

                    if i != UNITS - 4:
                        next_v()
                    transpose_p(g, i)
                    if i == UNITS - 4:
                        next_v()
                    next_qk()
                    values(g, i)
                    if not first:
                        router_step(g, i)
                output_rows(g, last)

            transpose_z(0, False)
            pe.wait_ge(s_consts, 1)
            pe.wait_ge(s_before0, 1)
            pe.wait_ge(s_r_lo, 1)
            pe.wait_ge(s_zl, DC)
            for j in range(4):
                if j >= 2:
                    pe.wait_ge(s_qkl, j - 1)
                project_qk(0, j)
                if j:
                    pe.wait_ge(s_ve, j)
                project_v(0, j)
                if j == 1:
                    scores(0, 0, False)
            group(0, True, False)
            with pe.Fori(1, GROUPS - 1) as g:
                group(g, False, False)
            group(GROUPS - 1, False, True)
            pe.wait_ge(s_woe, 2 * GROUPS + FREE_W)
            for i in range(UNITS):
                if i > 0:
                    router_bank_read(GROUPS, i)
                router_step(GROUPS, i)

        @block.scalar
        def _(act):
            act.sem_inc(s_pA, FREE_B)

            def exps(g, i, h):
                u = UNITS * g + i
                if h == 0:
                    act.wait_ge(s_T, 2 * u + 2)
                act.wait_ge(s_max, 2 * u + h + 1)
                for qt in range(2):
                    n = 2 * h + qt
                    m = act.activation(prob[u_par(i)][:, h, qt, 1:N], s_ps[h][:, qt * N + 1:(qt + 1) * N], ACT.Exp,
                                       bias=nmax[u_par(i)][:, n:n + 1], accum_out=rsum[u_par(i)][:, n:n + 1])
                m.then_inc(s_exp, 1)

            def qk_hi(g, j):
                act.wait_ge(s_qk, UNITS * g + j + 1)
                act.activation(qk[(j // 2) % 2][j % 2][0][:], proj_ps[j % 2][:], ACT.Copy).then_inc(s_qkh, 1)

            def z_hi(g):
                for c in range(DC):
                    act.wait_ge(s_zt, DC * g + c + 1)
                    act.activation(zT_hi[:, c, :], proj_ps[c][:], ACT.Copy).then_inc(s_zh, 1)

            def probT_a(g, i):
                act.wait_ge(s_T, 2 * (UNITS * g + i) + 1 + FREE_P)
                act.activation(probT[u_par(i)][:, 0, :, :], pT_ps[0][:].rearrange("p (k q) -> p k q", k=2),
                               ACT.Copy).then_inc(s_pA, 1)

            def o_hi(g, i):
                act.wait_ge(s_o, UNITS * g + i + 1)
                act.activation(oT_hi[:, i // 2, (i % 2) * N:(i % 2 + 1) * N], o_ps[:, 0:N], ACT.Copy).then_inc(s_oh, 1)

            def router_step(g, i):
                r, ps = g - 1, proj_ps[(i + 1) % 2]
                if i in (3, 4):
                    act.wait_ge(s_zt2, DC * r + i - 2)
                    act.activation(z2T_hi[:, i - 3, :], ps[:], ACT.Copy).then_inc(s_zh2, 1)
                elif i == 5:
                    act.wait_ge(s_lg, r + 1)
                    act.activation(logitsT[:], ps[:], ACT.Copy).then_inc(s_lgs, 1)
                elif i == 7:
                    act.wait_ge(s_nm, r + 1)
                    for t in range(GT):
                        act.activation(expo[:, t, 0:E], logits[:, t, 0:E], ACT.Exp, bias=row_nmax[:, t:t + 1],
                                       accum_out=esum[:, t:t + 1])
                    act.activation(expo[:, :, E:E + 1], logits[:, :, E:E + 1], ACT.Exp, scale=-1.0).then_inc(s_ex, 1)

            def group(g, first, last):
                for i in range(UNITS):
                    nxt = (g, i + 1) if i + 1 < UNITS else (g + 1, 0)
                    has_next = i + 1 < UNITS or not last
                    tile = (g + (i + 4) // UNITS, (i + 4) % UNITS)
                    has_tile = i + 4 < UNITS or not last
                    if i == UNITS - 4 and not last:
                        z_hi(g + 1)
                    if has_next:
                        exps(*nxt, 0)
                    probT_a(g, i)
                    if has_next:
                        exps(*nxt, 1)
                    if has_tile:
                        qk_hi(*tile)
                    o_hi(g, i)
                    if not first:
                        router_step(g, i)

            z_hi(0)
            act.wait_ge(s_r_in, 32)
            act.activation(r_hi[:], r_pad[:], ACT.Copy).then_inc(s_r_hi, 1)
            act.wait_ge(s_mask, 2)
            for j in range(4):
                qk_hi(0, j)
                if j == 1:
                    exps(0, 0, 0)
                    exps(0, 0, 1)
            group(0, True, False)
            with act.Fori(1, GROUPS - 1) as g:
                group(g, False, False)
            group(GROUPS - 1, False, True)
            for i in range(UNITS):
                router_step(GROUPS, i)
            fill_up(act, range(1, E, 2))

        @block.vector
        def _(dve):
            dve.sem_inc(s_pB, FREE_B)
            dve.sem_inc(s_ol, FREE_B)
            dve.sem_inc(s_woe, FREE_W)
            for i in range(2):
                dve.memset(prob[i][:, :, :, 0:1], 0.0).then_inc(s_mask, 1)

            def layernorm_stats(g, t):
                dve.bn_stats(stats[:, t, :], resid[:, GT * g + t, :]).then_inc(s_st, 1)
                dve.wait_ge(s_st, GT * g + t + 1)
                dve.sem_inc(s_go, 1)
                dve.bn_aggr(mean_var[:, t, :], stats[:, t, :]).then_inc(s_mv, 1)

            def layernorm_apply(g, t):
                dve.wait_ge(s_rstd, g + 1)
                dve.tensor_scalar(z[:, t, :], resid[:, GT * g + t, :], mean_var[:, t, 0:1], rstd[:, t:t + 1],
                                  ALU.subtract, ALU.mult).then_inc(s_z, 1)

            def maxima(g, i):
                for h in range(2):
                    dve.wait_ge(s_S, 2 * (UNITS * g + i) + h + 1)
                    dve.tensor_reduce(nmax[u_par(i)][:, 2 * h:2 * h + 2],
                                      s_ps[h][:].rearrange("p (q k) -> p q k", q=2)[:, :, 1:N], AX_X, ALU.max,
                                      negate=True).then_inc(s_max, 1)

            def qk_lo(g, j):
                hi, lo = qk[(j // 2) % 2][j % 2]
                dve.wait_ge(s_qkh, UNITS * g + j + 1)
                dve.tensor_tensor(lo[:], proj_ps[j % 2][:], f32(hi[:]), ALU.subtract).then_inc(s_qkl, 1)

            def z_lo(g):
                for c in range(DC):
                    dve.wait_ge(s_zh, DC * g + c + 1)
                    dve.tensor_tensor(zT_lo[:, c, :], proj_ps[c][:], f32(zT_hi[:, c, :]), ALU.subtract).then_inc(s_zl, 1)

            def v_copy(g, j):
                dve.wait_ge(s_v, UNITS * g + j + 1)
                dve.tensor_copy(v[(j // 4) % 2][:, j % 4, :], v_ps[:, 0:2 * P]).then_inc(s_ve, 1)

            def normalise_a(g, i):
                u, k = UNITS * g + i, u_par(i)
                dve.wait_ge(s_exp, 2 * u + 2)
                dve.tensor_scalar(rsum_eps[:], rsum[k][:], EPS_SM, None, ALU.add).then_inc(s_sum, 1)
                dve.wait_ge(s_sum, u + 1)
                dve.reciprocal(rinv[k][:], rsum_eps[:]).then_inc(s_rinv, 1)
                dve.wait_ge(s_rinv, u + 1)
                for qt in range(2):
                    m = dve.tensor_scalar(prob[k][:, 0, qt, 1:N], prob[k][:, 0, qt, 1:N], rinv[k][:, qt:qt + 1], None,
                                          ALU.mult)
                m.then_inc(s_nA, 1)

            def probT_b(g, i):
                dve.wait_ge(s_T, 2 * (UNITS * g + i) + 2 + FREE_P)
                dve.tensor_copy(probT[u_par(i)][:, 1, :, :],
                                pT_ps[1][:].rearrange("p (k q) -> p k q", k=2)).then_inc(s_pB, 1)

            def o_lo(g, i):
                part = slice((i % 2) * N, (i % 2 + 1) * N)
                dve.wait_ge(s_oh, UNITS * g + i + 1)
                dve.tensor_tensor(oT_lo[:, i // 2, part], o_ps[:, 0:N], f32(oT_hi[:, i // 2, part]),
                                  ALU.subtract).then_inc(s_ol, 1)

            def add_rows(g):
                dve.wait_ge(s_bias, GT * g + GT)
                for j in range(2):
                    rows = resid[:, bass.ds(GT * g + 2 * j, 2), :]
                    dve.wait_ge(s_wo, 2 * g + j + 1)
                    dve.tensor_tensor(rows, proj_ps[j][:].rearrange("p (t d) -> p t d", t=2), rows,
                                      ALU.add).then_inc(s_woe, 1)

            def after(ins, sem, steps, r, n):
                ins.then_inc(sem, 1)
                dve.wait_ge(sem, steps * r + n)
                dve.sem_inc(s_go, 1)


            def probabilities(r):
                dve.wait_ge(s_ex, r + 1)
                dve.tensor_scalar(gate_den[:], expo[:, :, E:E + 1], 1.0, None, ALU.add)
                after(dve.reciprocal(einv[:], esum[:]), s_chain, CHOICE_STEPS, r, 1)
                for t in range(GT):
                    m = dve.tensor_scalar(probs[:, t, :], expo[:, t, 0:E], einv[:, t:t + 1], None, ALU.mult)
                after(m, s_chain, CHOICE_STEPS, r, 2)
                for t in range(GT):
                    m = dve.max(top[:, t, :], probs[:, t, :])
                after(m, s_chain, CHOICE_STEPS, r, 3)

            def best_two(r):
                for t in range(GT):
                    m = dve.max_index(top_at[:, t, :], top[:, t, :], probs[:, t, :])
                m.then_inc(s_chain, 1)
                here = bass.ds(GT * r, GT)
                dve.tensor_copy(shares[:, here, 0:TOP], top[:, :, 0:TOP])
                dve.reciprocal(shares[:, here, TOP:TOP + 1], gate_den[:])
                dve.wait_ge(s_chain, CHOICE_STEPS * r + 4)
                after(dve.tensor_copy(top_f[:], top_at[:]), s_chain, CHOICE_STEPS, r, 5)

            def one_hot(r):
                for n in range(TOP):
                    for t in range(GT):
                        m = dve.tensor_scalar(hot[:, n, t, :], iota[:], top_f[:, t, n:n + 1], None, ALU.is_equal)
                after(m, s_chain, CHOICE_STEPS, r, 6)
                dve.tensor_tensor(taken[:], hot[:, 0], hot[:, 1], ALU.add).then_inc(s_taken, 1)


            def places(r):
                after(dve.tensor_copy(run[:, 0, :], run[:, GT, :]), s_chain2, PLACE_STEPS, r, 1)
                dve.wait_ge(s_rank_read, r + 1)
                for t in range(GT):
                    after(dve.tensor_tensor(run[:, t + 1, :], ranks[:, 1, t, :], run[:, t, :], ALU.add),
                          s_chain2, PLACE_STEPS, r, t + 2)
                dve.tensor_tensor(place[:], ranks[:, 0], run[:, 0:GT, :], ALU.add).then_inc(s_placed, 1)

            def row_slots(r):
                dve.wait_ge(s_placed, r + 1)
                for n in range(TOP):
                    m = dve.tensor_tensor(picked[:, n], hot[:, n], place[:], ALU.mult)
                after(m, s_chain2, PLACE_STEPS, r, GT + 2)
                for n in range(TOP):
                    m = dve.tensor_reduce(slot_f[:, :, n], picked[:, n], AX_X, ALU.add)
                after(m, s_chain2, PLACE_STEPS, r, GT + 3)
                dve.tensor_copy(slot_now[:], slot_f[:]).then_inc(s_slot, 1)
                dve.tensor_copy(slots_in[:, bass.ds(GT * r, GT), :], slot_f[:])

            def router_banks(g, i):
                r, ps = g - 1, proj_ps[i % 2]
                if i in (4, 5):
                    c = i - 4
                    dve.wait_ge(s_zh2, DC * r + c + 1)
                    dve.tensor_tensor(z2T_lo[:, c, :], ps[:], f32(z2T_hi[:, c, :]), ALU.subtract).then_inc(s_zl2, 1)
                elif i == 7:
                    dve.wait_ge(s_lt, r + 1)
                    dve.tensor_copy(logits[:], ps[:].rearrange("p (t e) -> p t e", t=GT)[:, :, 0:E + 1]).then_inc(s_lr, 1)
                    dve.wait_ge(s_lr, r + 1)
                    dve.tensor_reduce(row_nmax[:], logits[:, :, 0:E], AX_X, ALU.max, negate=True).then_inc(s_nm, 1)
                elif i == 11:
                    dve.wait_ge(s_rank, r + 1)
                    dve.tensor_copy(ranks[:].rearrange("p a t e -> p (a t e)"), ps[:, 0:2 * GT * E]).then_inc(s_rank_read, 1)

            def router_rows(g, i):
                r = g - 1
                if i in (0, 1):
                    dve.wait_ge(s_woe, 2 * r + i + 1 + FREE_W)
                    for t in (2 * i, 2 * i + 1):
                        dve.bn_stats(stats2[:, t, :], resid[:, GT * r + t, :]).then_inc(s_st2, 1)
                    for t in (2 * i, 2 * i + 1):
                        dve.wait_ge(s_st2, GT * r + t + 1)
                        dve.sem_inc(s_go, 1)
                        dve.bn_aggr(mean_var2[:, t, :], stats2[:, t, :]).then_inc(s_mv2, 1)
                elif i == 2:
                    dve.wait_ge(s_z2_free, r + 1)
                    dve.wait_ge(s_rstd2, r + 1)
                    for t in range(GT):
                        dve.tensor_scalar(z2[:, t, :], resid[:, GT * r + t, :], mean_var2[:, t, 0:1], rstd2[:, t:t + 1],
                                          ALU.subtract, ALU.mult).then_inc(s_z2, 1)
                elif 8 <= i < 13:
                    (probabilities, best_two, one_hot, places, row_slots)[i - 8](r)

            def tables():
                step = [0]

                def done(ins):
                    step[0] += 1
                    ins.then_inc(s_table, 1)
                    dve.wait_ge(s_table, step[0])
                    dve.sem_inc(s_go, 1)

                dve.tensor_copy(fill[:], run[0:1, GT, :]).then_inc(s_tail, 1)
                done(dve.scalar_tensor_tensor(out=tiles_f[:], in0=iota[:], scalar=-float(CAP), in1=run[:, GT, :],
                                              op0=ALU.mult, op1=ALU.add))
                done(dve.tensor_scalar(tiles_u[:], tiles_f[:], float(P - 1), None, ALU.add))
                done(dve.tensor_scalar(tiles_u[:], tiles_u[:], SHIFT, None, ALU.logical_shift_right))
                done(dve.tensor_copy(tiles_f[:], tiles_u[:]))
                dve.tensor_scalar(skips[:], tiles_f[:], -float(P), float(CAP), ALU.mult, ALU.add)
                dve.tensor_scalar(rows_f[:], turn_f[:], float(P), None, ALU.mult)
                done(dve.tensor_copy(ends[:, 0:1], tiles_f[0:1, 0:1]))
                for e in range(1, E):
                    done(dve.tensor_tensor(ends[:, e:e + 1], ends[:, e - 1:e], tiles_f[0:1, e:e + 1], ALU.add))
                for e in range(E):
                    dve.tensor_scalar(past[:, e, :], turn_f[:], ends[:, e:e + 1], None, ALU.is_ge)
                    m = dve.tensor_scalar(past_rows[:, e, :], turn_f[:], ends[:, e:e + 1], skips[0:1, e:e + 1],
                                          ALU.is_ge, ALU.mult)
                done(m)
                dve.tensor_reduce(table_e[:], past.rearrange("a e t -> a t e"), AX_X, ALU.add)
                done(dve.tensor_reduce(table_r[:], past_rows.rearrange("a e t -> a t e"), AX_X, ALU.add))
                dve.tensor_scalar(table_e[:], table_e[:], float(E - 1), None, ALU.min)
                done(dve.tensor_tensor(table_r[:], table_r[:], rows_f[:], ALU.add))
                dve.tensor_scalar(tile_in[:], table_r[:, 0:TILES], float(E * CAP), None, ALU.min)
                done(dve.tensor_tensor(past_rows[:, 0, 0:TILES], table_e[:, 0:TILES],
                                       place_value[:].rearrange("a w k -> a (w k)"), ALU.mult))
                done(dve.tensor_reduce(words[:], past_rows[:, 0, 0:TILES].rearrange("a (w k) -> a w k", k=HALF), AX_X, ALU.add))
                dve.scalar_tensor_tensor(out=tile_expert[:],
                                         in0=table_e[:, HALF:].rearrange("a (w k) -> a w k", k=HALF)[:, :, 0],
                                         scalar=float(E ** HALF), in1=words[:], op0=ALU.mult, op1=ALU.add)
                all_slots = slots_in[:].rearrange("p t k -> p (t k)")
                for e in range(1, E):
                    m = dve.tensor_scalar(passed[:, e - 1, :], all_slots, float(e * CAP), skips[:, e - 1:e],
                                          ALU.is_ge, ALU.mult)
                done(m)
                done(dve.tensor_reduce(skipped[:], passed.rearrange("p e n -> p n e"), AX_X, ALU.add))
                dve.tensor_tensor(slots[:].rearrange("p t k -> p (t k)"), all_slots, skipped[:], ALU.subtract)

            def group(g, first, last):
                for i in range(UNITS):
                    nxt = (g, i + 1) if i + 1 < UNITS else (g + 1, 0)
                    has_next = i + 1 < UNITS or not last
                    tile = (g + (i + 4) // UNITS, (i + 4) % UNITS)
                    has_tile = i + 4 < UNITS or not last
                    if i == UNITS - 4 and not last:
                        z_lo(g + 1)
                    if has_next:
                        maxima(*nxt)
                    if has_tile and i != UNITS - 4:
                        v_copy(*tile)
                    if not first:
                        router_banks(g, i)
                    probT_b(g, i)
                    if not first:
                        router_rows(g, i)
                    if not last and 3 <= i < 3 + GT:
                        layernorm_stats(g + 1, i - 3)
                    if not last and 8 <= i < 8 + GT:
                        layernorm_apply(g + 1, i - 8)
                    if has_tile and i == UNITS - 4:
                        v_copy(*tile)
                    if has_next:
                        normalise_a(*nxt)
                    if has_tile:
                        qk_lo(*tile)
                    o_lo(g, i)
                add_rows(g)

            dve.memset(ones[:], 1.0).then_inc(s_consts, 1)
            for k in range(HALF):
                dve.memset(place_value[:, :, k:k + 1], float(E ** k))
            for t in range(GT):
                layernorm_stats(0, t)
            for t in range(GT):
                layernorm_apply(0, t)
            z_lo(0)
            dve.wait_ge(s_r_hi, 1)
            dve.tensor_tensor(r_lo[:], r_pad[:], f32(r_hi[:]), ALU.subtract).then_inc(s_r_lo, 1)
            dve.wait_ge(s_iotas, 2)
            dve.tensor_copy(iota[:], iota_u[:])
            dve.tensor_copy(turn_f[:], turn_u[:])
            dve.tensor_scalar(run[:, GT, :], iota_u[:], float(CAP), None, ALU.mult)
            for j in range(4):
                qk_lo(0, j)
                v_copy(0, j)
                if j == 1:
                    maxima(0, 0)
                    normalise_a(0, 0)
            group(0, True, False)
            with dve.Fori(1, GROUPS - 1) as g:
                group(g, False, False)
            group(GROUPS - 1, False, True)
            for i in range(UNITS):
                router_banks(GROUPS, i)
                router_rows(GROUPS, i)
            tables()

        @block.gpsimd
        def _(pool):
            pool.memset(r_pad[:], 0.0).then_inc(s_r_zero, 1)
            pool.iota(iota_u[:], pattern=[[1, E]], base=0, channel_multiplier=0).then_inc(s_iotas, 1)
            pool.iota(turn_u[:], pattern=[[1, TILES + HALF]], base=0, channel_multiplier=0).then_inc(s_iotas, 1)
            pool.wait_ge(s_consts, 1)
            pool.affine_select(out=before[:], in_=ones[:], compare_op=ALU.is_gt, fill=0.0, base=0, pattern=[[1, P]],
                               channel_multiplier=-1).then_inc(s_before0, 1)

            def layernorm_rstd(g):
                pool.wait_ge(s_mv, GT * g + GT)
                pool.sem_inc(s_pgo, 1)
                pool.tensor_scalar(var_eps[:], mean_var[:, :, 1], EPS_LN, None, ALU.add).then_inc(s_var, 1)
                pool.wait_ge(s_var, g + 1)
                pool.tensor_tensor(rstd[:], var_eps[:], half_neg[:], ALU.pow).then_inc(s_rstd, 1)

            def add_bias(g, t):
                pool.wait_ge(s_z, GT * g + t + 1)
                rows = resid[:, GT * g + t, :]
                pool.tensor_tensor(rows, rows, bo_row[:], ALU.add).then_inc(s_bias, 1)

            def normalise_b(g, i):
                k = u_par(i)
                pool.wait_ge(s_rinv, UNITS * g + i + 1)
                pool.sem_inc(s_pgo, 1)
                for qt in range(2):
                    m = pool.tensor_scalar(prob[k][:, 1, qt, 1:N], prob[k][:, 1, qt, 1:N], rinv[k][:, 2 + qt:3 + qt],
                                           None, ALU.mult)
                m.then_inc(s_nB, 1)

            def router_step(g, i):
                r = g - 1
                if i == 1:
                    pool.wait_ge(s_mv2, GT * r + GT)
                    pool.sem_inc(s_pgo, 1)
                    pool.tensor_scalar(var_eps2[:], mean_var2[:, :, 1], EPS_LN, None, ALU.add).then_inc(s_var2, 1)
                    pool.wait_ge(s_var2, r + 1)
                    pool.tensor_tensor(rstd2[:], var_eps2[:], half_neg[:], ALU.pow).then_inc(s_rstd2, 1)
                elif i >= UNITS - GT:
                    t = i - (UNITS - GT)
                    for n in range(TOP * t, TOP * t + TOP):
                        if n == 0:
                            pool.wait_ge(s_slot, r + 1)
                            pool.sem_inc(s_pgo, 1)
                        pool.indirect_dma_start(
                            x_slots, bass.IndirectOffsetOnAxis(ap=slot_now[:, n // TOP, n % TOP:n % TOP + 1], axis=0),
                            z2[:, n // TOP, :], None).then_inc(s_scat, 16)

            def group(g, first, last):
                for i in range(UNITS):
                    if i + 1 < UNITS:
                        normalise_b(g, i + 1)
                    elif not last:
                        normalise_b(g + 1, 0)
                    if not first:
                        router_step(g, i)
                    if i == 3 + GT and not last:
                        layernorm_rstd(g + 1)
                    if 9 <= i < 9 + GT and not last:
                        add_bias(g + 1, i - 9)

            layernorm_rstd(0)
            pool.wait_ge(s_bo, 16)
            normalise_b(0, 0)
            for t in range(GT):
                add_bias(0, t)
            group(0, True, False)
            with pool.Fori(1, GROUPS - 1) as g:
                group(g, False, False)
            group(GROUPS - 1, False, True)
            for i in range(UNITS):
                router_step(GROUPS, i)
            pool.wait_ge(s_scat, 16 * GROUPS * GT * TOP)


def u_par(i):
    return i % 2


def expert_phase(nc, w1, w2, gate_up, down, out, resid, ident, slots, shares, tile_tables, z_dram, x_slots, y_slots):
    tile_expert, tile_in = tile_tables
    UNROLL = 2 * HALF
    TURNS = TILES // UNROLL
    BUFS = 4
    USES = UNROLL // BUFS
    BY_POOL = 2
    with ExitStack() as ctx:
        def sb(name, shape, dt=F32):
            return ctx.enter_context(nc.sbuf_tensor(name, shape, dt))

        def bank(name):
            return ctx.enter_context(nc.psum_tensor(name, [P, 512], F32))

        def sem(name):
            return ctx.enter_context(nc.semaphore(name))

        raw_up, raw_down = sb("raw_up", [P, DC, E, F]), sb("raw_down", [P, FC, E, D])
        raw_gu, raw_sd = sb("raw_gu", [P, DC, 2 * F]), sb("raw_sd", [P, FC, D])
        up_hi, up_lo = (sb(n, [P, DC, E, F], F32R) for n in ("up_hi", "up_lo"))
        dn_hi, dn_lo = (sb(n, [P, FC, E, D], F32R) for n in ("dn_hi", "dn_lo"))
        gu_hi, gu_lo = (sb(n, [P, DC, 2 * F], F32R) for n in ("gu_hi", "gu_lo"))
        sd_hi, sd_lo = (sb(n, [P, FC, D], F32R) for n in ("sd_hi", "sd_lo"))
        xg = [sb(f"xg{k}", [P, D]) for k in range(BUFS)]
        xgT_hi, xgT_lo = ([sb(f"{n}{k}", [P, DC * P], F32R) for k in range(2)] for n in ("xgT_hi", "xgT_lo"))
        hg = [sb(f"hg{k}", [P, F]) for k in range(2)]
        hgT_hi, hgT_lo = ([sb(f"{n}{k}", [P, FC * P], F32R) for k in range(2)] for n in ("hgT_hi", "hgT_lo"))
        yg = [sb(f"yg{k}", [P, D]) for k in range(BUFS)]
        z = sb("z3", [P, GT, D])
        zT_hi, zT_lo = (sb(n, [P, DC, GR], F32R) for n in ("z3T_hi", "z3T_lo"))
        h_full = sb("h_full", [P, FC, GR])
        h_hi, h_lo = (sb(n, [P, FC, GR], F32R) for n in ("h_hi", "h_lo"))
        back = sb("back", [P, GT, TOP, D])
        slot_now = sb("slot_now2", [P, GT, TOP], U32)
        share_now = sb("share_now", [P, GT, TOP])
        gate_now = sb("gate_now", [P, GT, 1])
        xT_ps, hg_ps, hT_ps, y_ps = ([bank(f"{n}{k}") for k in range(2)] for n in ("xgT_ps", "hg_ps", "hgT_ps", "y_ps"))
        gate_ps, up_ps = hg_ps, hT_ps

        s_raw = [sem(f"expert{e}_in") for e in range(E)]
        s_raw_gu = sem("shared_in")
        s_w_hi, s_w, s_half, s_gu_w = sem("expert_hi"), sem("expert_split"), sem("expert_hi_by_pool"), sem("shared_split")
        s_x_in = [sem(f"xg{k}_in") for k in range(BUFS)]
        s_xT, s_xh, s_xl = sem("xgT_in_psum"), sem("xgT_hi_ready"), sem("xgT_lo_ready")
        s_up, s_h = sem("hg_in_psum"), sem("hg_ready")
        s_hT, s_hh, s_hl = sem("hgT_in_psum"), sem("hgT_hi_ready"), sem("hgT_lo_ready")
        s_y, s_yc = sem("yg_in_psum"), sem("yg_ready")
        s_st = [sem(f"yg{k}_stored") for k in range(BUFS)]
        s_z_in, s_zt, s_zh, s_zl = sem("z3_in"), sem("z3T_in_psum"), sem("z3T_hi_ready"), sem("z3T_lo_ready")
        s_gu, s_silu, s_prod = sem("hidden_in_psum"), sem("silu_ready"), sem("gated_ready")
        s_hhi, s_hlo = sem("h_hi_ready"), sem("h_lo_ready")
        s_rows, s_all, s_out = sem("shared_rows_in_psum"), sem("rows_complete"), sem("out_stored")
        s_back = [sem(f"back{t}_in") for t in range(GT)]
        s_stored, s_idx, s_first, s_used = sem("all_yg_stored"), sem("slot_now_ready"), sem("first_added"), sem("back_used")
        s_share, s_gate = sem("share_now_ready"), sem("gate_now_ready")
        s_pgo = sem("pool_wait_met2")
        FREE_D = 16

        def load_expert(eng, e):
            eng.dma_start(raw_up[:, :, e, :], w1[e].rearrange("(c p) f -> p c f", p=P)).then_inc(s_raw[e], 16)
            eng.dma_start(raw_down[:, :, e, :], w2[e].rearrange("(c p) d -> p c d", p=P)).then_inc(s_raw[e], 16)

        def uses(r, k):
            return USES * r + k // BUFS

        block = ctx.enter_context(nc.Block())

        @block.sync
        def _(sp):
            def load(r, k, first):
                n = UNROLL * r + k
                if not first:
                    sp.wait_ge(s_xT, n - BUFS + 1)
                at = sp.value_load(tile_in[0:1, bass.ds(n, 1)], min_val=0, max_val=E * CAP)
                sp.dma_start(xg[k % BUFS][:], x_slots[bass.ds(at, P), :]).then_inc(s_x_in[k % BUFS], 16)

            def store(r, k):
                n = UNROLL * r + k
                sp.wait_ge(s_yc, n + 1)
                sp.dma_start(y_slots[bass.ds(P * n, P), :], yg[k % BUFS][:]).then_inc(s_st[k % BUFS], 16)

            def store_group(g):
                sp.wait_ge(s_all, GT * g + GT)
                rows = resid[:, bass.ds(GT * g, GT), :].rearrange("p (b h) d -> p b h d", h=2)
                sp.dma_start(out[bass.ds(2 * g, 2), 0:P - 1, :].rearrange("b p d -> p b d"),
                             rows[1:P, :, 0, :]).then_inc(s_out, 16)
                sp.dma_start(out[bass.ds(2 * g, 2), P - 1:N - 1, :].rearrange("b p d -> p b d"),
                             rows[:, :, 1, :]).then_inc(s_out, 16)

            for k in range(BUFS):
                sp.sem_inc(s_st[k], FREE_D)
            load_expert(sp, 0)
            for k in range(BUFS):
                load(0, k, True)

            def turn(r, last):
                for k in range(UNROLL):
                    if k + BUFS < UNROLL or not last:
                        load(r + (k + BUFS) // UNROLL, (k + BUFS) % UNROLL, False)
                    store(r, k)

            with sp.Fori(0, TURNS - 1) as r:
                turn(r, False)
            sp.dma_start(z[:], z_dram[0]).then_inc(s_z_in, 16)
            turn(TURNS - 1, True)
            for k in range(BUFS):
                sp.wait_ge(s_st[k], 16 * TURNS * USES + FREE_D)
            sp.sem_inc(s_stored, 1)
            sp.wait_ge(s_zt, DC)
            sp.dma_start(z[:], z_dram[1]).then_inc(s_z_in, 16)
            with sp.Fori(2, GROUPS) as g:
                sp.wait_ge(s_zt, DC * g)
                sp.dma_start(z[:], z_dram[bass.ds(g, 1)].rearrange("a p t d -> p (a t) d")).then_inc(s_z_in, 16)
                store_group(g - 2)
            store_group(GROUPS - 2)
            store_group(GROUPS - 1)
            sp.wait_ge(s_out, 32 * GROUPS)


        @block.tensor
        def _(pe):
            def transpose_x(r, k, first):
                n = UNROLL * r + k
                pe.wait_ge(s_x_in[k % BUFS], 16 * (uses(r, k) + 1))
                if not first:
                    pe.wait_ge(s_xl, n - 1)
                for c in range(DC):
                    m = pe.transpose(xT_ps[k % 2][:, c * P:(c + 1) * P], xg[k % BUFS][:, c * P:(c + 1) * P], ident[:])
                m.then_inc(s_xT, 1)

            def experts_of(r, half):
                word = pe.value_load(tile_expert[0:1, bass.ds(2 * r + half, 1)], min_val=0, max_val=E ** (HALF + 1) - 1)
                return [(word >> (BITS * k)) & (E - 1) for k in range(HALF + 1)]

            def up(r, k, e, first):
                n = UNROLL * r + k
                pe.wait_ge(s_w, e + 1)
                pe.wait_ge(s_xl, n + 1)
                if not first:
                    pe.wait_ge(s_h, n - 1)
                for c in range(DC):
                    cols = slice(c * P, (c + 1) * P)
                    m = three(pe, hg_ps[k % 2][:, 0:F], xgT_hi[k % 2][:, cols], xgT_lo[k % 2][:, cols],
                              up_hi[:, c, bass.ds(e, 1), :], up_lo[:, c, bass.ds(e, 1), :], c == 0, c == DC - 1)
                m.then_inc(s_up, 1)

            def transpose_h(r, k, first):
                n = UNROLL * r + k
                pe.wait_ge(s_h, n + 1)
                if not first:
                    pe.wait_ge(s_hl, n - 1)
                for c in range(FC):
                    m = pe.transpose(hT_ps[k % 2][:, c * P:(c + 1) * P], hg[k % 2][:, c * P:(c + 1) * P], ident[:])
                m.then_inc(s_hT, 1)

            def down_rows(r, k, e, first):
                n = UNROLL * r + k
                pe.wait_ge(s_hl, n + 1)
                if not first:
                    pe.wait_ge(s_yc, n - 1)
                for c in range(FC):
                    cols = slice(c * P, (c + 1) * P)
                    m = three(pe, y_ps[k % 2][:, 0:D], hgT_hi[k % 2][:, cols], hgT_lo[k % 2][:, cols],
                              dn_hi[:, c, bass.ds(e, 1), :], dn_lo[:, c, bass.ds(e, 1), :], c == 0, c == FC - 1)
                m.then_inc(s_y, 1)

            def turn(r, first, last):
                e = experts_of(r, 0)
                for k in range(UNROLL):
                    transpose_h(r, k, first and k < 2)
                    if k + 1 < UNROLL or not last:
                        up(r + (k + 1) // UNROLL, (k + 1) % UNROLL, e[k + 1], first and k + 1 < 2)
                    if k + 2 < UNROLL or not last:
                        transpose_x(r + (k + 2) // UNROLL, (k + 2) % UNROLL, False)
                    down_rows(r, k, e[k], first and k < 2)
                    if k == HALF - 2:
                        e = e[:HALF] + experts_of(r, 1)

            transpose_x(0, 0, True)
            transpose_x(0, 1, True)
            up(0, 0, experts_of(0, 0)[0], True)
            turn(0, True, False)
            with pe.Fori(1, TURNS - 1) as r:
                turn(r, False, False)
            turn(TURNS - 1, False, True)

            def transpose_z(g):
                pe.wait_ge(s_z_in, 16 * (g + 1))
                for c in range(DC):
                    for t in range(GT):
                        m = pe.transpose(xT_ps[c][:, t * P:(t + 1) * P], z[:, t, c * P:(c + 1) * P], ident[:])
                    m.then_inc(s_zt, 1)

            def shared_hidden(g, first):
                pe.wait_ge(s_zl, DC * g + DC)
                for c2 in range(FC):
                    if not first:
                        pe.wait_ge(s_prod, FC * g - 1 + c2)
                    for k, ps in enumerate((gate_ps[c2], up_ps[c2])):
                        cols = slice(k * F + c2 * P, k * F + (c2 + 1) * P)
                        for c in range(DC):
                            m = three(pe, ps[:], gu_hi[:, c, cols], gu_lo[:, c, cols], zT_hi[:, c, :], zT_lo[:, c, :],
                                      c == 0, c == DC - 1)
                        m.then_inc(s_gu, 1)

            def shared_rows(g, first):
                pe.wait_ge(s_hlo, FC * g + FC)
                for half in range(2):
                    if not first:
                        pe.wait_ge(s_all, GT * (g - 1) + 2 * half + 2)
                    for t in (2 * half, 2 * half + 1):
                        rows = slice(t * P, (t + 1) * P)
                        for c in range(FC):
                            m = three(pe, y_ps[half][:, (t % 2) * D:(t % 2 + 1) * D], h_hi[:, c, rows], h_lo[:, c, rows],
                                      sd_hi[:, c, :], sd_lo[:, c, :], c == 0, c == FC - 1)
                    m.then_inc(s_rows, 1)

            pe.wait_ge(s_xl, TILES)
            transpose_z(0)
            pe.wait_ge(s_gu_w, 1)
            shared_hidden(0, True)
            transpose_z(1)
            shared_hidden(1, False)
            transpose_z(2)
            pe.wait_ge(s_yc, TILES)
            shared_rows(0, True)
            with pe.Fori(2, GROUPS - 1) as g:
                shared_hidden(g, False)
                transpose_z(g + 1)
                shared_rows(g - 1, False)
            shared_hidden(GROUPS - 1, False)
            shared_rows(GROUPS - 2, False)
            shared_rows(GROUPS - 1, False)

        @block.scalar
        def _(act):
            def split_hi(e):
                act.wait_ge(s_raw[e], 32)
                act.activation(up_hi[:, :, e, :], raw_up[:, :, e, :], ACT.Copy).then_inc(s_w_hi, 1)
                act.activation(dn_hi[:, :, e, :], raw_down[:, :, e, :], ACT.Copy).then_inc(s_w_hi, 1)

            def x_hi(r, k, first):
                n = UNROLL * r + k
                act.wait_ge(s_xT, n + 1)
                if not first:
                    act.wait_ge(s_up, n - 1)
                act.activation(xgT_hi[k % 2][:], xT_ps[k % 2][:, 0:DC * P], ACT.Copy).then_inc(s_xh, 1)

            def silu(r, k, first):
                n = UNROLL * r + k
                act.wait_ge(s_up, n + 1)
                if not first:
                    act.wait_ge(s_hT, n - 1)
                act.activation(hg[k % 2][:], hg_ps[k % 2][:, 0:F], ACT.Silu).then_inc(s_h, 1)

            def hidden_hi(r, k, first):
                n = UNROLL * r + k
                act.wait_ge(s_hT, n + 1)
                if not first:
                    act.wait_ge(s_y, n - 1)
                act.activation(hgT_hi[k % 2][:], hT_ps[k % 2][:, 0:FC * P], ACT.Copy).then_inc(s_hh, 1)

            def turn(r, first, last):
                for k in range(UNROLL):
                    hidden_hi(r, k, first and k < 2)
                    if k + 1 < UNROLL or not last:
                        silu(r + (k + 1) // UNROLL, (k + 1) % UNROLL, first and k + 1 < 2)
                    if k + 2 < UNROLL or not last:
                        x_hi(r + (k + 2) // UNROLL, (k + 2) % UNROLL, False)

            for e in range(1, BY_POOL):
                load_expert(act, e)
            split_hi(0)
            x_hi(0, 0, True)
            x_hi(0, 1, True)
            silu(0, 0, True)
            split_hi(1)
            turn(0, True, False)
            with act.Fori(1, TURNS - 1) as r:
                turn(r, False, False)
            turn(TURNS - 1, False, True)

            def z_hi(g):
                for c in range(DC):
                    act.wait_ge(s_zt, DC * g + c + 1)
                    act.activation(zT_hi[:, c, :], xT_ps[c][:], ACT.Copy).then_inc(s_zh, 1)

            def shared_silu(g, first):
                for c in range(FC):
                    act.wait_ge(s_gu, 2 * FC * g + 2 * c + 1)
                    if not first:
                        act.wait_ge(s_hlo, FC * g - 1 + c)
                    act.activation(h_full[:, c, :], gate_ps[c][:], ACT.Silu).then_inc(s_silu, 1)

            def shared_hi(g, first):
                if not first:
                    act.wait_ge(s_rows, 2 * g)
                for c in range(FC):
                    act.wait_ge(s_prod, FC * g + c + 1)
                    act.activation(h_hi[:, c, :], h_full[:, c, :], ACT.Copy).then_inc(s_hhi, 1)

            z_hi(0)
            shared_silu(0, True)
            z_hi(1)
            shared_hi(0, True)
            with act.Fori(1, GROUPS - 1) as g:
                shared_silu(g, False)
                z_hi(g + 1)
                shared_hi(g, False)
            shared_silu(GROUPS - 1, False)
            shared_hi(GROUPS - 1, False)

        @block.vector
        def _(dve):
            def split_lo(e):
                for n, (lo, raw, hi) in enumerate(((up_lo, raw_up, up_hi), (dn_lo, raw_down, dn_hi))):
                    dve.wait_ge(s_w_hi, 2 * e + n + 1)
                    m = dve.tensor_tensor(lo[:, :, e, :], raw[:, :, e, :], f32(hi[:, :, e, :]), ALU.subtract)
                m.then_inc(s_w, 1)

            def x_lo(r, k):
                n = UNROLL * r + k
                dve.wait_ge(s_xh, n + 1)
                dve.tensor_tensor(xgT_lo[k % 2][:], xT_ps[k % 2][:, 0:DC * P], f32(xgT_hi[k % 2][:]),
                                  ALU.subtract).then_inc(s_xl, 1)

            def hidden_lo(r, k):
                n = UNROLL * r + k
                dve.wait_ge(s_hh, n + 1)
                dve.tensor_tensor(hgT_lo[k % 2][:], hT_ps[k % 2][:, 0:FC * P], f32(hgT_hi[k % 2][:]),
                                  ALU.subtract).then_inc(s_hl, 1)

            def y_copy(r, k):
                n = UNROLL * r + k
                dve.wait_ge(s_y, n + 1)
                dve.wait_ge(s_st[k % BUFS], 16 * uses(r, k) + FREE_D)
                dve.tensor_copy(yg[k % BUFS][:], y_ps[k % 2][:, 0:D]).then_inc(s_yc, 1)

            def turn(r, first, last):
                for k in range(UNROLL):
                    hidden_lo(r, k)
                    if k + 2 < UNROLL or not last:
                        x_lo(r + (k + 2) // UNROLL, (k + 2) % UNROLL)
                    y_copy(r, k)

            split_lo(0)
            x_lo(0, 0)
            x_lo(0, 1)
            split_lo(1)
            turn(0, True, False)
            with dve.Fori(1, TURNS - 1) as r:
                turn(r, False, False)
            turn(TURNS - 1, False, True)

            def z_lo(g):
                for c in range(DC):
                    dve.wait_ge(s_zh, DC * g + c + 1)
                    dve.tensor_tensor(zT_lo[:, c, :], xT_ps[c][:], f32(zT_hi[:, c, :]), ALU.subtract).then_inc(s_zl, 1)

            def product(g, c):
                dve.wait_ge(s_silu, FC * g + c + 1)
                dve.wait_ge(s_gu, 2 * FC * g + 2 * c + 2)
                dve.tensor_tensor(h_full[:, c, :], up_ps[c][:], h_full[:, c, :], ALU.mult).then_inc(s_prod, 1)

            def shared_lo(g):
                for c in range(FC):
                    dve.wait_ge(s_hhi, FC * g + c + 1)
                    dve.tensor_tensor(h_lo[:, c, :], h_full[:, c, :], f32(h_hi[:, c, :]), ALU.subtract).then_inc(s_hlo, 1)

            def add_back(g, t):
                if t == 0:
                    dve.tensor_copy(share_now[:], shares[:, bass.ds(GT * g, GT), 0:TOP]).then_inc(s_share, 1)
                    dve.wait_ge(s_share, g + 1)
                rows = resid[:, GT * g + t, :]
                dve.wait_ge(s_back[t], 16 * TOP * (g + 1))
                dve.scalar_tensor_tensor(out=rows, in0=back[:, t, 0, :], scalar=share_now[:, t, 0:1], in1=rows,
                                         op0=ALU.mult, op1=ALU.add).then_inc(s_first, 1)
                dve.wait_ge(s_first, GT * g + t + 1)
                dve.scalar_tensor_tensor(out=rows, in0=back[:, t, 1, :], scalar=share_now[:, t, 1:2], in1=rows,
                                         op0=ALU.mult, op1=ALU.add).then_inc(s_used, 1)

            def add_shared(g):
                dve.tensor_copy(gate_now[:], shares[:, bass.ds(GT * g, GT), TOP:TOP + 1]).then_inc(s_gate, 1)
                dve.wait_ge(s_gate, g + 1)
                for half in range(2):
                    dve.wait_ge(s_rows, 2 * g + half + 1)
                    dve.wait_ge(s_used, GT * g + 2 * half + 2)
                    for t in (2 * half, 2 * half + 1):
                        rows = resid[:, GT * g + t, :]
                        dve.scalar_tensor_tensor(out=rows, in0=y_ps[half][:, (t % 2) * D:(t % 2 + 1) * D],
                                                 scalar=gate_now[:, t, :], in1=rows, op0=ALU.mult,
                                                 op1=ALU.add).then_inc(s_all, 1)

            def group(g, first, last):
                product(g, 0)
                if not first:
                    add_back(g - 1, 2)
                product(g, 1)
                if not first:
                    add_back(g - 1, 3)
                if not last:
                    z_lo(g + 1)
                if not first:
                    add_shared(g - 1)
                add_back(g, 0)
                shared_lo(g)
                add_back(g, 1)

            z_lo(0)
            group(0, True, False)
            with dve.Fori(1, GROUPS - 1) as g:
                group(g, False, False)
            group(GROUPS - 1, False, True)
            add_back(GROUPS - 1, 2)
            add_back(GROUPS - 1, 3)
            add_shared(GROUPS - 1)

        @block.gpsimd
        def _(pool):
            for e in range(BY_POOL, E):
                load_expert(pool, e)
            pool.dma_start(raw_gu[:], gate_up.rearrange("(c p) f -> p c f", p=P)).then_inc(s_raw_gu, 16)
            pool.dma_start(raw_sd[:], down.rearrange("(c p) d -> p c d", p=P)).then_inc(s_raw_gu, 16)

            def split(n, parts, ready):
                for raw, hi, _ in parts:
                    m = pool.tensor_copy(hi, raw)
                m.then_inc(s_half, 1)
                pool.wait_ge(s_half, n + 1)
                for raw, hi, lo in parts:
                    m = pool.tensor_tensor(lo, raw, f32(hi), ALU.subtract)
                m.then_inc(ready, 1)

            for n, e in enumerate(range(BY_POOL, E)):
                pool.wait_ge(s_raw[e], 32)
                if n == 0:
                    pool.wait_ge(s_w, BY_POOL)
                split(n, [(raw_up[:, :, e, :], up_hi[:, :, e, :], up_lo[:, :, e, :]),
                          (raw_down[:, :, e, :], dn_hi[:, :, e, :], dn_lo[:, :, e, :])], s_w)
            pool.wait_ge(s_raw_gu, 32)
            split(E - BY_POOL, [(raw_gu[:], gu_hi[:], gu_lo[:]), (raw_sd[:], sd_hi[:], sd_lo[:])], s_gu_w)

            def gather(g, t, first):
                n = GT * g + t
                if not first:
                    pool.wait_ge(s_used, n - GT + 1)
                pool.tensor_copy(slot_now[:, t, :], slots[:, n, :]).then_inc(s_idx, 1)
                pool.wait_ge(s_idx, n + 1)
                pool.sem_inc(s_pgo, 1)
                for k in range(TOP):
                    pool.indirect_dma_start(back[:, t, k, :], None, y_slots,
                                            bass.IndirectOffsetOnAxis(ap=slot_now[:, t, k:k + 1], axis=0)
                                            ).then_inc(s_back[t], 16)

            pool.wait_ge(s_stored, 1)
            for t in range(GT):
                gather(0, t, True)
            with pool.Fori(1, GROUPS) as g:
                for t in range(GT):
                    gather(g, t, False)


_INS = ["x", "L0_tok_W", "L0_tok_b", "L0_attn_Wq", "L0_attn_Wk", "L0_attn_Wv", "L0_attn_Wo", "L0_attn_bo",
        "L0_ffn_router_w", "L0_ffn_w1", "L0_ffn_w2", "L0_ffn_shared_gate_up", "L0_ffn_shared_down",
        "L0_ffn_shared_gate_w"]
_OUT = ((B, N - 1, D), "float32")


def kernel(**inputs):
    import numpy as _np
    import concourse.bacc as _bacc
    from concourse import mybir as _mybir
    from concourse.bass_utils import run_bass_kernel_spmd as _run

    nc = _bacc.Bacc("TRN2", target_bir_lowering=False, num_devices=1)
    arrays, args = {}, []
    for name in _INS:
        a = _np.ascontiguousarray(inputs[name])
        arrays[f"in_{name}_dram"] = a
        args.append(nc.dram_tensor(f"in_{name}_dram", a.shape, _mybir.dt.from_np(a.dtype), kind="ExternalInput").ap())
    out = nc.dram_tensor("out_0_dram", _OUT[0], _mybir.dt.from_np(_np.dtype(_OUT[1])), kind="ExternalOutput").ap()
    build(nc, *args, out)
    r = _run(nc, [arrays], core_ids=[0])
    return r.results[0]["out_0_dram"]
```
